# Optimizing a Trainium2 kernel written in Bass

```python
import numpy as np
import jax
import jax.numpy as jnp

def _softmax(x, axis=-1):
    return jax.nn.softmax(x, axis=axis)

def _gelu(x):
    return jax.nn.gelu(x, approximate=True)

def _silu(x):
    return jax.nn.silu(x)

def _sigmoid(x):
    return jax.nn.sigmoid(x)

def _layernorm(x, axis=-1, eps=1e-05):
    m = jnp.mean(x, axis=axis, keepdims=True)
    v = jnp.var(x, axis=axis, keepdims=True)
    return (x - m) / jnp.sqrt(v + eps)

def _scatter_add(tgt, idx, src, axis=0):
    return tgt.at[idx].add(src)

def _segment_sum(src, seg, n):
    return jax.ops.segment_sum(src, seg, n)
kernel_name = 'mk_decoder_postln_d1_seqx_r8_4d1f5e'

def setup_inputs(seed: int=0):
    np.random.seed(seed)
    _w = jnp.asarray

    def _rec_inputs():
        import jax
        import jax.numpy as jnp
        _rk = jax.random.key(seed)
        x = 7.22e-05 + 1 * jax.random.normal(jax.random.fold_in(_rk, 1), (32, 128, 128), jnp.float32)
        _lenS = 128 - jax.random.randint(jax.random.fold_in(_rk, 7), (32,), 0, max(1, 128 // 4) + 1, jnp.int32)
        _lenS2 = 128 - jax.random.randint(jax.random.fold_in(_rk, 8), (32,), 0, max(1, 128 // 4) + 1, jnp.int32)
        _ctx_1024P = jax.random.normal(jax.random.fold_in(_rk, 11), (32, 16, 128), jnp.float32)
        _ctx_1024c = jax.random.dirichlet(jax.random.fold_in(_rk, 511), 0.3 * jnp.ones((16,), jnp.float32), (32, 128))
        _ctx_1024t = jnp.einsum('bsk,bkd->bsd', _ctx_1024c, _ctx_1024P)
        _ctx_1024t = _ctx_1024t * jax.lax.rsqrt(jnp.mean(jnp.square(_ctx_1024t)) + 1e-12) * 0.953939
        ctx_1024 = 4.13588e-05 + 0.999923 * (_ctx_1024t + 0.3 * jax.random.normal(jax.random.fold_in(_rk, 611), (32, 128, 128), jnp.float32))
        _validS = jnp.arange(128)[None, :] < _lenS[:, None]
        _validS2 = jnp.arange(128)[None, :] < _lenS2[:, None]
        _causal = jnp.tril(jnp.ones((128, 128), dtype=bool))
        mask_BxS2_bf1 = jnp.ones((32, 128), dtype=bool)
        mask_BxS2_bk0 = jnp.logical_not(jnp.broadcast_to(_validS2[:, :], (32, 128)))
        return (x, ctx_1024, mask_BxS2_bf1, mask_BxS2_bk0)
    x, ctx_1024, mask_BxS2_bf1, mask_BxS2_bk0 = _rec_inputs()

    def _L0_attn_setup():
        import jax, jax.numpy as jnp
        import numpy as np
        from math import sqrt
        ROPE_BASE = 6000.0

        def _rope_tables(seq_len, rope_dim, dtype):
            inv_freq = 1.0 / ROPE_BASE ** (jnp.arange(0, rope_dim, 2, dtype=jnp.float32) / rope_dim)
            t = jnp.arange(seq_len, dtype=jnp.float32)
            freqs = jnp.outer(t, inv_freq)
            emb = jnp.concatenate([freqs, freqs], axis=-1)
            return (jnp.cos(emb).astype(dtype), jnp.sin(emb).astype(dtype))

        def _rotate_half(x):
            x1, x2 = jnp.split(x, 2, axis=-1)
            return jnp.concatenate([-x2, x1], axis=-1)
        key = jax.random.key(seed)
        k1, k2, k3 = jax.random.split(key, 3)
        B, S, D = (2, 256, 128)
        H, DK = (16, 64)
        x = jax.random.normal(k1, (B, S, D), dtype=jnp.float32)
        W_qkv = jax.random.normal(k2, (3, H, DK, D), dtype=jnp.float32) * 0.02
        W_o = jax.random.normal(k3, (D, H * DK), dtype=jnp.float32) * 0.02
        return {'x': x, 'W_qkv': W_qkv, 'W_o': W_o}
    _L0_attn_all = _L0_attn_setup()
    _L0_attn_in = {k: v for k, v in _L0_attn_all.items() if k in ('W_qkv', 'W_o')}
    del _L0_attn_all

    def _L0_xattn_setup():
        import jax, jax.numpy as jnp
        import numpy as np
        D_MODEL = 128
        N_HEADS = 16
        NUM_KV_HEADS = 4
        D_K = D_MODEL // N_HEADS
        ROPE_BASE = 10000.0

        def _apply_rope(x, dim, base=ROPE_BASE, position_offset=0):
            T = x.shape[2]
            dtype = x.dtype
            theta = base ** (-jnp.arange(0, dim, 2, dtype=dtype) / dim)
            positions = jnp.arange(position_offset, position_offset + T, dtype=dtype)[:, None]
            angles = positions * theta[None, :]
            sin = jnp.sin(angles)[None, None]
            cos = jnp.cos(angles)[None, None]
            x1 = x[..., :dim // 2]
            x2 = x[..., dim // 2:dim]
            return jnp.concatenate([x1 * cos - x2 * sin, x1 * sin + x2 * cos], axis=-1)
        key = jax.random.key(seed)
        ks = jax.random.split(key, 7)
        B, Tq, Tkv = (4, 256, 256)
        s = 1.0 / np.sqrt(D_MODEL)
        return {'query': jax.random.normal(ks[0], (B, Tq, D_MODEL), jnp.float32), 'key_value': jax.random.normal(ks[1], (B, Tkv, D_MODEL), jnp.float32), 'query_mask': jnp.ones((B, Tq), dtype=bool), 'kv_mask': jax.random.randint(ks[2], (B, Tkv), 0, 2) > 0, 'w_q': jax.random.normal(ks[3], (D_MODEL, D_MODEL), jnp.float32) * s, 'w_k': jax.random.normal(ks[4], (D_MODEL, NUM_KV_HEADS * D_K), jnp.float32) * s, 'w_v': jax.random.normal(ks[5], (D_MODEL, NUM_KV_HEADS * D_K), jnp.float32) * s, 'w_out': jax.random.normal(ks[6], (D_MODEL, D_MODEL), jnp.float32) * s}
    _L0_xattn_all = _L0_xattn_setup()
    _L0_xattn_in = {k: v for k, v in _L0_xattn_all.items() if k in ('w_q', 'w_k', 'w_v', 'w_out')}
    del _L0_xattn_all

    def _L0_ffn_setup():
        import jax, jax.numpy as jnp
        import numpy as np
        B, T, D, E, FF, K = (4, 128, 128, 8, 256, 2)
        SINKHORN_ITERS = 3

        def _sinkhorn(log_alpha, iters=SINKHORN_ITERS):
            for _ in range(iters):
                log_alpha = log_alpha - jax.nn.logsumexp(log_alpha, axis=-1, keepdims=True)
                log_alpha = log_alpha - jax.nn.logsumexp(log_alpha, axis=-2, keepdims=True)
            gates = jnp.exp(log_alpha)
            return gates / (jnp.sum(gates, axis=-1, keepdims=True) + 1e-08)
        key = jax.random.key(seed)
        ks = jax.random.split(key, 7)
        scale = 0.02
        return {'x': jax.random.normal(ks[0], (B, T, D), dtype=jnp.float32), 'router_w': jax.random.normal(ks[1], (E, D), dtype=jnp.float32) * scale, 'router_b': jnp.zeros((E,), dtype=jnp.float32), 'temperature': jnp.ones((1,), dtype=jnp.float32) * 0.5, 'wg': jax.random.normal(ks[2], (E, D, FF), dtype=jnp.float32) * scale, 'wp': jax.random.normal(ks[3], (E, D, FF), dtype=jnp.float32) * scale, 'wo': jax.random.normal(ks[4], (E, FF, D), dtype=jnp.float32) * scale}
    _L0_ffn_all = _L0_ffn_setup()
    _L0_ffn_in = {k: v for k, v in _L0_ffn_all.items() if k in ('router_w', 'router_b', 'temperature', 'wg', 'wp', 'wo')}
    del _L0_ffn_all
    return {'x': x, 'ctx_1024': ctx_1024, 'mask_BxS2_bf1': mask_BxS2_bf1, 'mask_BxS2_bk0': mask_BxS2_bk0, 'L0_attn_W_qkv': _L0_attn_in['W_qkv'], 'L0_attn_W_o': _L0_attn_in['W_o'], 'L0_xattn_w_q': _L0_xattn_in['w_q'], 'L0_xattn_w_k': _L0_xattn_in['w_k'], 'L0_xattn_w_v': _L0_xattn_in['w_v'], 'L0_xattn_w_out': _L0_xattn_in['w_out'], 'L0_ffn_router_w': _L0_ffn_in['router_w'], 'L0_ffn_router_b': _L0_ffn_in['router_b'], 'L0_ffn_temperature': _L0_ffn_in['temperature'], 'L0_ffn_wg': _L0_ffn_in['wg'], 'L0_ffn_wp': _L0_ffn_in['wp'], 'L0_ffn_wo': _L0_ffn_in['wo']}

def reference(x, ctx_1024, mask_BxS2_bf1, mask_BxS2_bk0, L0_attn_W_qkv, L0_attn_W_o, L0_xattn_w_q, L0_xattn_w_k, L0_xattn_w_v, L0_xattn_w_out, L0_ffn_router_w, L0_ffn_router_b, L0_ffn_temperature, L0_ffn_wg, L0_ffn_wp, L0_ffn_wo):
    import jax
    import jax.numpy as jnp

    def _L0_attn_ref(x, W_qkv, W_o):
        import jax, jax.numpy as jnp
        import numpy as np
        from math import sqrt
        ROPE_BASE = 6000.0

        def _rope_tables(seq_len, rope_dim, dtype):
            inv_freq = 1.0 / ROPE_BASE ** (jnp.arange(0, rope_dim, 2, dtype=jnp.float32) / rope_dim)
            t = jnp.arange(seq_len, dtype=jnp.float32)
            freqs = jnp.outer(t, inv_freq)
            emb = jnp.concatenate([freqs, freqs], axis=-1)
            return (jnp.cos(emb).astype(dtype), jnp.sin(emb).astype(dtype))

        def _rotate_half(x):
            x1, x2 = jnp.split(x, 2, axis=-1)
            return jnp.concatenate([-x2, x1], axis=-1)
        B, S, D = x.shape
        _, H, DK, _ = W_qkv.shape
        rope_dim = DK // 2
        qkv = jnp.einsum('bsm,qhdm->bqhsd', x, W_qkv)
        cos, sin = _rope_tables(S, rope_dim, x.dtype)
        qk = qkv[:, :2, :, :, :rope_dim]
        qk_rot = qk * cos + _rotate_half(qk) * sin
        qkv = qkv.at[:, :2, :, :, :rope_dim].set(qk_rot)
        Q, K, V = (qkv[:, 0], qkv[:, 1], qkv[:, 2])
        scores = jnp.einsum('bhqd,bhkd->bhqk', Q, K)
        causal = jnp.triu(jnp.ones((S, S), dtype=bool), k=1)
        scores = jnp.where(causal, -jnp.inf, scores) / sqrt(DK)
        attn = jax.nn.softmax(scores, axis=-1)
        out = jnp.einsum('bhqk,bhkd->bhqd', attn, V)
        out = out.transpose(0, 2, 1, 3).reshape(B, S, H * DK)
        return jnp.einsum('bsh,dh->bsd', out, W_o)

    def _L0_xattn_ref(query, key_value, query_mask, kv_mask, w_q, w_k, w_v, w_out):
        import jax, jax.numpy as jnp
        import numpy as np
        D_MODEL = 128
        N_HEADS = 16
        NUM_KV_HEADS = 4
        D_K = D_MODEL // N_HEADS
        ROPE_BASE = 10000.0

        def _apply_rope(x, dim, base=ROPE_BASE, position_offset=0):
            T = x.shape[2]
            dtype = x.dtype
            theta = base ** (-jnp.arange(0, dim, 2, dtype=dtype) / dim)
            positions = jnp.arange(position_offset, position_offset + T, dtype=dtype)[:, None]
            angles = positions * theta[None, :]
            sin = jnp.sin(angles)[None, None]
            cos = jnp.cos(angles)[None, None]
            x1 = x[..., :dim // 2]
            x2 = x[..., dim // 2:dim]
            return jnp.concatenate([x1 * cos - x2 * sin, x1 * sin + x2 * cos], axis=-1)
        B, Tq, _ = query.shape
        Tkv = key_value.shape[1]
        group = N_HEADS // NUM_KV_HEADS
        Q = (query @ w_q).reshape(B, Tq, N_HEADS, D_K).transpose(0, 2, 1, 3)
        K = (key_value @ w_k).reshape(B, Tkv, NUM_KV_HEADS, D_K).transpose(0, 2, 1, 3)
        V = (key_value @ w_v).reshape(B, Tkv, NUM_KV_HEADS, D_K).transpose(0, 2, 1, 3)
        K = _apply_rope(K, D_K)
        Q = _apply_rope(Q, D_K)
        K = jnp.repeat(K, group, axis=1)
        V = jnp.repeat(V, group, axis=1)
        attn_mask = kv_mask[:, None, None, :] & query_mask[:, None, :, None]
        scale = 1.0 / jnp.sqrt(jnp.asarray(D_K, Q.dtype))
        scores = jnp.einsum('bhqd,bhkd->bhqk', Q, K) * scale
        scores = jnp.where(attn_mask, scores, jnp.finfo(scores.dtype).min)
        probs = jax.nn.softmax(scores, axis=-1)
        out = jnp.einsum('bhqk,bhkd->bhqd', probs, V)
        out = out.transpose(0, 2, 1, 3).reshape(B, Tq, D_MODEL)
        return out @ w_out

    def _L0_ffn_ref(x, router_w, router_b, temperature, wg, wp, wo):
        import jax, jax.numpy as jnp
        import numpy as np
        B, T, D, E, FF, K = (4, 128, 128, 8, 256, 2)
        SINKHORN_ITERS = 3

        def _sinkhorn(log_alpha, iters=SINKHORN_ITERS):
            for _ in range(iters):
                log_alpha = log_alpha - jax.nn.logsumexp(log_alpha, axis=-1, keepdims=True)
                log_alpha = log_alpha - jax.nn.logsumexp(log_alpha, axis=-2, keepdims=True)
            gates = jnp.exp(log_alpha)
            return gates / (jnp.sum(gates, axis=-1, keepdims=True) + 1e-08)
        temp = jnp.maximum(temperature, 0.1)
        scores = (jnp.einsum('btd,ed->bte', x, router_w) + router_b) / temp
        gates = _sinkhorn(scores)
        topk_vals, topk_idx = jax.lax.top_k(gates, K)
        topk_gates = topk_vals / (jnp.sum(topk_vals, axis=-1, keepdims=True) + 1e-08)
        g = jax.nn.relu(jnp.einsum('btd,edf->btef', x, wg))
        p = jnp.einsum('btd,edf->btef', x, wp)
        all_out = jnp.einsum('btef,efd->bted', g * p, wo)
        gathered = jnp.take_along_axis(all_out, topk_idx[..., None], axis=2)
        expert_out = jnp.sum(gathered * topk_gates[..., None], axis=2)
        return x + expert_out
    x = _layernorm(x + _L0_attn_ref(x, L0_attn_W_qkv, L0_attn_W_o), axis=-1)
    x = _layernorm(x + _L0_xattn_ref(x, ctx_1024, mask_BxS2_bf1, mask_BxS2_bk0, L0_xattn_w_q, L0_xattn_w_k, L0_xattn_w_v, L0_xattn_w_out), axis=-1)
    x = _layernorm(x + _L0_ffn_ref(x, L0_ffn_router_w, L0_ffn_router_b, L0_ffn_temperature, L0_ffn_wg, L0_ffn_wp, L0_ffn_wo), axis=-1)
    return x

_drawn_inputs = setup_inputs


def setup_inputs(seed=0):
    import zlib

    import numpy as np

    out = dict(_drawn_inputs(seed))
    spreads = {'L0_ffn_router_b': (0.0, 0.8)}
    factors = {'L0_ffn_router_w': 8.0, 'L0_ffn_wg': 8.0, 'L0_ffn_wp': 8.0, 'L0_ffn_wo': 8.0}
    for name, (base, spread) in spreads.items():
        noise = np.random.default_rng([zlib.crc32(name.encode()), seed]).standard_normal(out[name].shape)
        drawn = base * np.exp(spread * noise) if base else spread * noise
        out[name] = jnp.asarray(drawn.astype(out[name].dtype))
    for name, factor in factors.items():
        out[name] = (out[name] * factor).astype(out[name].dtype)
    return out
```

```python
from contextlib import ExitStack

import numpy as np
import concourse.bass as bass
from concourse import mybir

F32 = mybir.dt.float32
F32R = mybir.dt.float32r
BF16 = mybir.dt.bfloat16
U8 = mybir.dt.uint8
ALU = mybir.AluOpType
ACT = mybir.ActivationFunctionType
AX_X = mybir.AxisListType.X

B, S, D = 32, 128, 128
H, DK = 16, 64
ROPE = DK // 2
XH, XG, XK = 16, 4, 8
GRP = XH // XG
E, FF = 8, 256
QKV = 3 * H * DK
COLS = 512
CH = H * DK // D
EPS = 1e-5
CAUSAL = -1.0e30
BIG = float(2.0 ** 127)
FB = 4
SINKHORN_ITERS = 3


class Ring:

    def __init__(self, sem, name, banks, fills):
        self.banks = banks
        self.n = len(banks)
        self.per = [len(range(k, fills, self.n)) for k in range(self.n)]
        self.filled = [sem(f"{name}_filled{k}") for k in range(self.n)]
        self.drained = [sem(f"{name}_drained{k}") for k in range(self.n)]

    def bank(self, fill):
        return self.banks[fill % self.n]

    def count(self, b, fill):
        return b * self.per[fill % self.n] + fill // self.n + 1


def wait(eng, sem, value):
    if isinstance(value, int) and value <= 0:
        return
    eng.wait_ge(sem, value)


def decoder_layer(nc, x, ctx, qmask, kpad, cosq, sinq, xcos, xsin, ident_d, causal_d, wqkv, wo, xwq, xwkv, xwo,
                  rw, rb, temp, eidx, fwg, fwp, fwo, out):
    with ExitStack() as whole:
        def sem(name):
            return whole.enter_context(nc.semaphore(name))

        def keep(name, shape, dt=F32):
            return whole.enter_context(nc.sbuf_tensor(name, shape, dt))

        ps = whole.enter_context(nc.psum_tensor("ps", [128, 8, COLS], F32))
        x2_all = keep("x2_all", [128, B, D])
        x2T_hi = keep("x2T_hi", [128, B * S], F32R)
        x2T_lo = keep("x2T_lo", [128, B * S], F32R)
        logits = keep("logits", [128, B, E])
        ident = keep("ident", [128, 128])
        mhalf = keep("mhalf", [128, FB])
        scratch = keep("scratch", [128, 1])
        eps = keep("eps", [128, FB])

        attention_phase(nc, sem, ps, x2_all, x2T_hi, x2T_lo, logits, ident, mhalf, eps, scratch, x, ctx, qmask, kpad, cosq, sinq,
                        xcos, xsin, ident_d, causal_d, wqkv, wo, xwq, xwkv, xwo, rw, rb)
        ffn_phase(nc, sem, ps, x2_all, x2T_hi, x2T_lo, logits, ident, mhalf, eps, scratch, temp, eidx, fwg, fwp, fwo, out)


def attention_phase(nc, sem, ps, x2_all, x2T_hi, x2T_lo, logits, ident, mhalf, eps, scratch, x, ctx, qmask, kpad, cosq, sinq,
                    xcos, xsin, ident_d, causal_d, wqkv, wo, xwq, xwkv, xwo, rw, rb):
    with ExitStack() as phase:
        def sb(name, shape, dt=F32):
            return phase.enter_context(nc.sbuf_tensor(name, shape, dt))

        w_hi = sb("w_hi", [128, QKV], F32R)
        w_lo = sb("w_lo", [128, QKV], F32R)
        wo_sb = sb("wo_sb", [128, CH, D])
        xwq_sb = sb("xwq_sb", [128, XH * XK])
        xwkv_sb = sb("xwkv_sb", [128, 2 * XG * XK])
        xwo_sb = sb("xwo_sb", [128, D])
        rw_sb = sb("rw_sb", [128, E])
        rb_sb = sb("rb_sb", [128, E])
        identb = sb("identb", [128, 128], BF16)
        causal = sb("causal", [128, 4, 128], BF16)
        causal_f = sb("causal_f", [128, 128])
        cos_sb = sb("cos_sb", [128, ROPE])
        sin_sb = sb("sin_sb", [128, ROPE])
        xcos_sb = sb("xcos_sb", [128, XH + XG, XK])
        xsin_sb = sb("xsin_sb", [128, XH + XG, XK])
        qm_u8 = sb("qm_u8", [128, B], U8)
        kp_u8 = sb("kp_u8", [128, B], U8)
        qm_all = sb("qm_all", [128, B])
        kb_all = sb("kb_all", [128, B])
        xf = [sb(f"xf{p}", [128, D]) for p in range(2)]
        xT_hi = sb("xT_hi", [128, S], F32R)
        xT_lo = sb("xT_lo", [128, S], F32R)
        qk = sb("qk", [128, 2 * H, DK])
        qk_sin = sb("qk_sin", [128, 2 * H, ROPE])
        qT = [sb(f"qT{p}", [128, CH, S]) for p in range(2)]
        kT = [sb(f"kT{p}", [128, CH, S]) for p in range(2)]
        v = [sb(f"v{p}", [128, H * DK]) for p in range(2)]
        prob = sb("prob", [128, 4, 4, S])
        probT = sb("probT", [128, 4, 4, S])
        negmax = sb("negmax", [128, 4, 4])
        sums = sb("sums", [128, 4, 4])
        recip = sb("recip", [128, 4, 4])
        oT = sb("oT", [128, CH, S])
        xres = [sb(f"xres{p}", [128, D]) for p in range(2)]
        y1 = sb("y1", [128, D])
        st1 = sb("st1", [128, 6])
        mv1 = sb("mv1", [128, 2])
        ve1 = sb("ve1", [128, 1])
        rstd1 = sb("rstd1", [128, 1])
        x1 = [sb(f"x1{p}", [128, D]) for p in range(2)]
        x1c = [sb(f"x1c{p}", [128, D]) for p in range(2)]
        cx = [sb(f"cx{p}", [128, D]) for p in range(2)]
        xcT = sb("xcT", [128, 2, S])
        xt1 = sb("xt1", [128, XH + XG, XK])
        xt2 = sb("xt2", [128, XH + XG, XK])
        xqr = sb("xqr", [128, XH * XK])
        qm = sb("qm", [128, 1])
        kb = sb("kb", [128, 1])
        xq_pad = sb("xq_pad", [128, GRP, XG, 32])
        xk_pad = sb("xk_pad", [128, XG, 32])
        xqT = sb("xqT", [128, GRP, S])
        xkT = sb("xkT", [128, S])
        xv = [sb(f"xv{p}", [128, XG, 32]) for p in range(2)]
        xmax = sb("xmax", [128, XG, GRP])
        xprob = sb("xprob", [128, XG, GRP, S])
        xprobT = sb("xprobT", [128, XG, GRP, S])
        xoT = [sb(f"xoT{p}", [128, GRP, S]) for p in range(2)]
        xrec = sb("xrec", [128, GRP, XG])
        xo = sb("xo", [128, XH * XK])
        xonT = sb("xonT", [128, S])
        y2 = sb("y2", [128, D])
        st2 = sb("st2", [128, 6])
        mv2 = sb("mv2", [128, 2])
        ve2 = sb("ve2", [128, 1])
        rstd2 = sb("rstd2", [128, 1])
        x2 = sb("x2", [128, D])
        x2T = sb("x2T", [128, S])

        front = Ring(sem, "front", [0, 1], 11)
        F_XT, F_QKV, F_T = 0, 1, 7
        back = Ring(sem, "back", [2, 3, 4], 11)
        B_S, B_PT, B_OT, B_Y = 0, 4, 8, 10
        crossa = Ring(sem, "crossa", [5, 6], 13)
        A_T, A_QKV, A_QT, A_KT, A_S, A_PT, A_OT = 0, 1, 2, 3, 4, 8, 12
        crossb = Ring(sem, "crossb", [7], 5)
        C_O, C_T, C_Y, C_XT, C_R = range(5)

        w_loaded = sem("w_loaded")
        wqkv_loaded = sem("wqkv_loaded")
        const_ready = sem("const_ready")
        masks_made = sem("masks_made")
        w_hi_ready = sem("w_hi_ready")
        w_lo_ready = sem("w_lo_ready")
        xf_loaded = [sem(f"xf_loaded{p}") for p in range(2)]
        xres_loaded = [sem(f"xres_loaded{p}") for p in range(2)]
        cx_loaded = [sem(f"cx_loaded{p}") for p in range(2)]
        x_hi_ready = sem("x_hi_ready")
        sin_done = sem("sin_done")
        cos_done = sem("cos_done")
        roped = sem("roped")
        maxed = sem("maxed")
        summed = sem("summed")
        normed = sem("normed")
        st1_ready = sem("st1_ready")
        mv1_ready = sem("mv1_ready")
        ve1_ready = sem("ve1_ready")
        rstd1_ready = sem("rstd1_ready")
        x1_ready = sem("x1_ready")
        masks_ready = sem("masks_ready")
        xt1_ready = sem("xt1_ready")
        xt2_ready = sem("xt2_ready")
        xqr_ready = sem("xqr_ready")
        xpads_ready = sem("xpads_ready")
        xmaxed = sem("xmaxed")
        xexp = sem("xexp")
        xrec_ready = sem("xrec_ready")
        st2_ready = sem("st2_ready")
        mv2_ready = sem("mv2_ready")
        ve2_ready = sem("ve2_ready")
        rstd2_ready = sem("rstd2_ready")
        x2_ready = sem("x2_ready")
        x2_hi_ready = sem("x2_hi_ready")
        x2_split = sem("x2_split")

        small = [(wo_sb[:], wo.rearrange("(c p) n -> p c n", p=128)), (xwq_sb[:], xwq), (xwkv_sb[:], xwkv),
                 (xwo_sb[:], xwo), (rw_sb[:], rw), (rb_sb[:], rb), (cos_sb[:], cosq), (sin_sb[:], sinq),
                 (xcos_sb[:].rearrange("p h k -> p (h k)"), xcos), (xsin_sb[:].rearrange("p h k -> p (h k)"), xsin),
                 (qm_u8[:], qmask), (kp_u8[:], kpad), (causal_f[:], causal_d)]
        stage = [qk[:].rearrange("p h k -> p (h k)")[:, 0:QKV // 2], prob[:].rearrange("p a b c -> p (a b c)")[:, 0:QKV // 2]]

        def slots(eng, slot):
            for s in range(4):
                slot(s, s % 2, s, s - 1, s - 2, s - 3)
            with eng.Fori(2, B // 2) as turn:
                for p in range(2):
                    s = 2 * turn + p
                    slot(s, p, s, s - 1, s - 2, s - 3)
            for s in range(B, B + 3):
                slot(s, s % 2, s, s - 1, s - 2, s - 3)

        def loads(b, parity):
            return 8 * b + 16 - 8 * parity

        def on(b):
            return not isinstance(b, int) or 0 <= b < B

        block = phase.enter_context(nc.Block())

        @block.sync
        def _(sp):
            sp.dma_start(ident[:], ident_d).then_inc(wqkv_loaded, 16)
            for half in range(2):
                sp.dma_start(stage[half], wqkv[:, half * QKV // 2:(half + 1) * QKV // 2]).then_inc(wqkv_loaded, 16)

            def slot(s, p, f, k, a, c):
                if on(f):
                    wait(sp, front.filled[0], front.count(f - 2, F_XT) if not isinstance(f, int) or f >= 2 else 0)
                    sp.dma_start(xf[p][:], x[bass.ds(f, 1), :, :].rearrange("a s d -> s (a d)")).then_inc(xf_loaded[p], 16)
                    if isinstance(s, int) and s == 0:
                        for dst, src in small:
                            sp.dma_start(dst, src).then_inc(w_loaded, 16)
                    if not isinstance(f, int) or f >= 2:
                        wait(sp, back.drained[B_Y % back.n], back.count(f - 2, B_Y))
                    sp.dma_start(xres[p][:], x[bass.ds(f, 1), :, :].rearrange("a s d -> s (a d)")).then_inc(xres_loaded[p], 16)
                    if not isinstance(f, int) or f >= 2:
                        wait(sp, crossa.filled[0], crossa.count(f - 2, A_T))
                    sp.dma_start(cx[p][:], ctx[bass.ds(f, 1), :, :].rearrange("a s d -> s (a d)")).then_inc(cx_loaded[p], 16)

            slots(sp, slot)

        @block.gpsimd
        def _(pool):
            nc.gpsimd.memset(mhalf[:], -0.5)
            nc.gpsimd.memset(eps[:], EPS)
            nc.gpsimd.memset(xq_pad[:], 0.0)
            nc.gpsimd.memset(xk_pad[:], 0.0)
            for p in range(2):
                nc.gpsimd.memset(xv[p][:], 0.0).then_inc(const_ready, 1)
            pool.wait_ge(const_ready, 2)
            for p in range(2):
                nc.gpsimd.memset(xv[p][:, :, XK:XK + 1], 1.0).then_inc(const_ready, 1)

            def norm_fill(b, f):
                pool.wait_ge(summed, 4 * b + f + 1)
                nc.gpsimd.tensor_tensor(prob[:, f], prob[:, f], recip[:, f, :, None].broadcast_to([128, 4, S]),
                                        ALU.mult).then_inc(normed, 1)

            def rope_add(b, n):
                pool.wait_ge(cos_done, 4 * b + n + 1)
                part = qk[:, 8 * n:8 * n + 8, 0:ROPE]
                nc.gpsimd.tensor_tensor(part, part, qk_sin[:, 8 * n:8 * n + 8, :], ALU.add).then_inc(roped, 1)

            def rstd(b, mv, ve, out_, mv_ready, ve_ready, done):
                pool.wait_ge(mv_ready, b + 1)
                nc.gpsimd.tensor_tensor(ve[:], mv[:, 1:2], eps[:, 0:1], ALU.add).then_inc(ve_ready, 1)
                pool.wait_ge(ve_ready, b + 1)
                nc.gpsimd.tensor_tensor(out_[:], ve[:], mhalf[:, 0:1], ALU.pow).then_inc(done, 1)

            def slot(s, p, f, k, a, c):
                if on(k):
                    norm_fill(k, 0)
                    norm_fill(k, 1)
                if on(f):
                    rope_add(f, 0)
                    rope_add(f, 1)
                if on(k):
                    norm_fill(k, 2)
                    norm_fill(k, 3)
                if on(f):
                    rope_add(f, 2)
                    rope_add(f, 3)
                if on(c):
                    rstd(c, mv2, ve2, rstd2, mv2_ready, ve2_ready, rstd2_ready)
                if on(k):
                    rstd(k, mv1, ve1, rstd1, mv1_ready, ve1_ready, rstd1_ready)

            slots(pool, slot)

        @block.scalar
        def _(act):
            def copy(ring, b, fill, dst, src, scale=1.0):
                act.wait_ge(ring.filled[fill % ring.n], ring.count(b, fill))
                nc.scalar.activation(dst, src, ACT.Copy, scale=scale).then_inc(ring.drained[fill % ring.n], 1)

            def bank(ring, fill):
                return ps[:, ring.bank(fill), :]

            for half in range(2):
                act.wait_ge(wqkv_loaded, 16 * 3)
                nc.scalar.activation(w_hi[:, half * QKV // 2:(half + 1) * QKV // 2], stage[half],
                                     ACT.Copy).then_inc(w_hi_ready, 1)

            def exp_fill(b, f):
                act.wait_ge(maxed, 4 * b + f + 1)
                for j in range(4):
                    last = nc.scalar.activation(prob[:, f, j, :], bank(back, B_S + f)[:, j * S:(j + 1) * S], ACT.Exp,
                                                bias=negmax[:, f, j:j + 1], accum_out=sums[:, f, j:j + 1])
                last.then_inc(back.drained[(B_S + f) % back.n], 1)

            def xexp_fill(b, g):
                act.wait_ge(crossa.drained[(A_S + g) % 2], crossa.count(b, A_S + g))
                part = xprob[:, g].rearrange("p c s -> p (c s)")
                nc.scalar.activation(part, part, ACT.Exp).then_inc(xexp, 1)

            def q_copy(b, n):
                copy(front, b, F_QKV + n, qk[:, 8 * n:8 * n + 8, :].rearrange("p h k -> p (h k)"),
                     bank(front, F_QKV + n), DK ** -0.5 if n < 2 else 1.0)

            def probT_copy(b, f):
                copy(back, b, B_PT + f, probT[:, f].rearrange("p j s -> p (j s)"), bank(back, B_PT + f))

            def xprobT_copy(b, g):
                copy(crossa, b, A_PT + g, xprobT[:, g].rearrange("p j s -> p (j s)"), bank(crossa, A_PT + g))

            def slot(s, p, f, k, a, c):
                q = 1 - p
                if on(f):
                    if isinstance(s, int) and s == 0:
                        act.wait_ge(w_lo_ready, 2)
                    act.wait_ge(front.filled[0], front.count(f, F_XT))
                    nc.scalar.activation(xT_hi[:], bank(front, F_XT)[:, 0:S], ACT.Copy).then_inc(x_hi_ready, 1)
                if on(k):
                    for n in range(4):
                        exp_fill(k, n)
                if on(a):
                    copy(crossa, a, A_T, xcT[:].rearrange("p a s -> p (a s)"), bank(crossa, A_T)[:, 0:2 * S])
                if on(f):
                    q_copy(f, 0)
                    q_copy(f, 1)
                if on(c):
                    copy(crossb, c, C_T, xonT[:], bank(crossb, C_T)[:, 0:S])
                if on(f):
                    q_copy(f, 2)
                    q_copy(f, 3)
                if on(k):
                    probT_copy(k, 0)
                if on(a):
                    copy(crossa, a, A_QT, xqT[:].rearrange("p c s -> p (c s)"), bank(crossa, A_QT))
                    copy(crossa, a, A_KT, xkT[:], bank(crossa, A_KT)[:, 0:S])
                if on(k):
                    probT_copy(k, 2)
                if on(c):
                    wait(act, x2_split, c)
                    copy(crossb, c, C_XT, x2T[:], bank(crossb, C_XT)[:, 0:S])
                if on(a):
                    xexp_fill(a, 0)
                    xexp_fill(a, 1)
                if on(f):
                    for n in range(2):
                        copy(front, f, F_T + n, qT[p][:, 4 * n:4 * n + 4, :].rearrange("p c s -> p (c s)"),
                             bank(front, F_T + n))
                if on(a):
                    xexp_fill(a, 2)
                    xexp_fill(a, 3)
                    xprobT_copy(a, 0)
                    xprobT_copy(a, 2)
                    copy(crossa, a, A_OT, xoT[p][:].rearrange("p c s -> p (c s)"), bank(crossa, A_OT))

            slots(act, slot)

        @block.vector
        def _(dve):
            def bank(ring, fill):
                return ps[:, ring.bank(fill), :]

            def filled(ring, b, fill):
                dve.wait_ge(ring.filled[fill % ring.n], ring.count(b, fill))

            def copy(ring, b, fill, dst, src):
                filled(ring, b, fill)
                nc.vector.tensor_copy(dst, src).then_inc(ring.drained[fill % ring.n], 1)

            for half in range(2):
                dve.wait_ge(w_hi_ready, half + 1)
                part = slice(half * QKV // 2, (half + 1) * QKV // 2)
                nc.vector.tensor_tensor(w_lo[:, part], stage[half], w_hi[:, part].bitcast(F32),
                                        ALU.subtract).then_inc(w_lo_ready, 1)
            dve.wait_ge(w_loaded, 16 * len(small))
            nc.vector.tensor_copy(qm_all[:], qm_u8[:])
            nc.vector.tensor_copy(identb[:], ident[:])
            nc.vector.tensor_copy(causal[:], causal_f[:, None, :].broadcast_to([128, 4, 128]))
            nc.vector.tensor_scalar(kb_all[:], kp_u8[:], -1.0, BIG, ALU.add, ALU.mult).then_inc(masks_made, 1)
            dve.wait_ge(masks_made, 1)
            dve.wait_ge(const_ready, 4)

            def max_fill(b, f):
                filled(back, b, B_S + f)
                nc.vector.tensor_reduce(negmax[:, f, :], bank(back, B_S + f).rearrange("p (j s) -> p j s", j=4),
                                        AX_X, ALU.max, negate=True).then_inc(maxed, 1)

            def recip_fill(b, f):
                dve.wait_ge(back.drained[(B_S + f) % back.n], back.count(b, B_S + f))
                nc.vector.reciprocal(recip[:, f, :], sums[:, f, :]).then_inc(summed, 1)

            def rope_fill(b, n):
                dve.wait_ge(front.drained[(F_QKV + n) % 2], front.count(b, F_QKV + n))
                part = qk[:, 8 * n:8 * n + 8, 0:ROPE].rearrange("p h (a i) -> p h a i", a=2)
                sines = qk_sin[:, 8 * n:8 * n + 8, :].rearrange("p h (a i) -> p h a i", a=2)
                for side in range(2):
                    table = sin_sb[:, None, side * ROPE // 2:(side + 1) * ROPE // 2].broadcast_to([128, 8, ROPE // 2])
                    last = nc.vector.tensor_tensor(sines[:, :, side, :], part[:, :, 1 - side, :], table, ALU.mult)
                last.then_inc(sin_done, 1)
                dve.wait_ge(sin_done, 4 * b + n + 1)
                nc.vector.tensor_tensor(qk[:, 8 * n:8 * n + 8, 0:ROPE], qk[:, 8 * n:8 * n + 8, 0:ROPE],
                                        cos_sb[:, None, :].broadcast_to([128, 8, ROPE]), ALU.mult).then_inc(cos_done, 1)

            def layer_norm(b, y, st, mv, rs, kept, dst, ring, fill, st_ready, mv_ready, rs_ready, done):
                dve.wait_ge(ring.drained[fill % ring.n], ring.count(b, fill))
                nc.vector.bn_stats(st[:], y[:]).then_inc(st_ready, 1)
                dve.wait_ge(st_ready, b + 1)
                nc.vector.memset(scratch[:], 0.0)
                nc.vector.bn_aggr(mv[:], st[:]).then_inc(mv_ready, 1)
                dve.wait_ge(rs_ready, b + 1)
                for d in (kept, dst):
                    last = nc.vector.tensor_scalar(d, y[:], mv[:, 0:1], rs[:, 0:1], ALU.subtract, ALU.mult)
                last.then_inc(done, 1)

            def cross_qkv(b, p):
                nc.vector.tensor_copy(qm[:], qm_all[:, bass.ds(b, 1)])
                nc.vector.tensor_copy(kb[:], kb_all[:, bass.ds(b, 1)]).then_inc(masks_ready, 1)
                filled(crossa, b, A_QKV)
                src = bank(crossa, A_QKV)[:, 0:(XH + XG) * XK].rearrange("p (h a i) -> p h a i", a=2, i=XK // 2)
                t1 = xt1[:].rearrange("p h k -> p (h k)")
                nc.vector.tensor_tensor(t1, bank(crossa, A_QKV)[:, 0:(XH + XG) * XK],
                                        xcos_sb[:].rearrange("p h k -> p (h k)"), ALU.mult).then_inc(xt1_ready, 1)
                t2 = xt2[:].rearrange("p h (a i) -> p h a i", a=2)
                sn = xsin_sb[:].rearrange("p h (a i) -> p h a i", a=2)
                for side in range(2):
                    last = nc.vector.tensor_tensor(t2[:, :, side, :], src[:, :, 1 - side, :], sn[:, :, side, :], ALU.mult)
                last.then_inc(xt2_ready, 1)
                nc.vector.tensor_copy(xv[p][:, :, 0:XK],
                                      bank(crossa, A_QKV)[:, 160:192].rearrange("p (g k) -> p g k", g=XG))\
                    .then_inc(crossa.drained[A_QKV % 2], 1)
                dve.wait_ge(xt1_ready, b + 1)
                dve.wait_ge(xt2_ready, b + 1)
                nc.vector.tensor_tensor(xqr[:], xt1[:, 0:XH].rearrange("p h k -> p (h k)"),
                                        xt2[:, 0:XH].rearrange("p h k -> p (h k)"), ALU.add).then_inc(xqr_ready, 1)
                nc.vector.tensor_tensor(xk_pad[:, :, 0:XK], xt1[:, XH:XH + XG], xt2[:, XH:XH + XG],
                                        ALU.add).then_inc(xpads_ready, 1)
                dve.wait_ge(masks_ready, b + 1)
                nc.vector.tensor_copy(xk_pad[:, :, XK], kb[:, 0:1].broadcast_to([128, XG])).then_inc(xpads_ready, 1)
                nc.vector.tensor_copy(xq_pad[:, :, :, XK], qm[:, 0:1, None].broadcast_to([128, GRP, XG])).then_inc(xpads_ready, 1)
                dve.wait_ge(xqr_ready, b + 1)
                nc.vector.tensor_scalar(xq_pad[:, :, :, 0:XK].rearrange("p c g k -> p g c k"),
                                        xqr[:].rearrange("p (g c k) -> p g c k", g=XG, c=GRP), qm[:, 0:1], None,
                                        ALU.mult).then_inc(xpads_ready, 1)

            def xmax_fill(b, g):
                filled(crossa, b, A_S + g)
                src = bank(crossa, A_S + g).rearrange("p (j s) -> p j s", j=GRP)
                nc.vector.tensor_reduce(xmax[:, g, :], src, AX_X, ALU.max).then_inc(xmaxed, 1)
                dve.wait_ge(xmaxed, 4 * b + g + 1)
                nc.vector.tensor_tensor(xprob[:, g], src, xmax[:, g, :, None].broadcast_to([128, GRP, S]), ALU.subtract)\
                    .then_inc(crossa.drained[(A_S + g) % 2], 1)

            def slot(s, p, f, k, a, c):
                q = 1 - p
                if on(f):
                    dve.wait_ge(x_hi_ready, f + 1)
                    nc.vector.tensor_tensor(xT_lo[:], bank(front, F_XT)[:, 0:S], xT_hi[:].bitcast(F32),
                                            ALU.subtract).then_inc(front.drained[0], 1)
                if on(k):
                    max_fill(k, 0)
                    max_fill(k, 1)
                if on(c):
                    filled(crossb, c, C_O)
                    o = bank(crossb, C_O).rearrange("p (c g r) -> p c g r", c=GRP, g=XG)
                    nc.vector.reciprocal(xrec[:], o[:, :, :, XK]).then_inc(xrec_ready, 1)
                    dve.wait_ge(xrec_ready, c + 1)
                    nc.vector.tensor_tensor(xo[:].rearrange("p (g c k) -> p c g k", g=XG, c=GRP), o[:, :, :, 0:XK],
                                            xrec[:, :, :, None].broadcast_to([128, GRP, XG, XK]), ALU.mult)\
                        .then_inc(crossb.drained[0], 1)
                if on(k):
                    max_fill(k, 2)
                    recip_fill(k, 0)
                    max_fill(k, 3)
                    recip_fill(k, 1)
                if on(f):
                    rope_fill(f, 0)
                    rope_fill(f, 1)
                if on(k):
                    recip_fill(k, 2)
                    recip_fill(k, 3)
                if on(f):
                    rope_fill(f, 2)
                    rope_fill(f, 3)
                if on(a):
                    cross_qkv(a, p)
                if on(k):
                    copy(back, k, B_PT + 1, probT[:, 1].rearrange("p j s -> p (j s)"), bank(back, B_PT + 1))
                if on(c):
                    filled(crossb, c, C_Y)
                    nc.vector.tensor_tensor(y2[:], bank(crossb, C_Y)[:, 0:D], x1c[q][:], ALU.add)\
                        .then_inc(crossb.drained[0], 1)
                    layer_norm(c, y2, st2, mv2, rstd2, x2_all[:, bass.ds(c, 1), :].rearrange("p a d -> p (a d)"),
                               x2[:], crossb, C_Y, st2_ready, mv2_ready, rstd2_ready, x2_ready)
                if on(f):
                    for n in range(2):
                        copy(front, f, F_QKV + 4 + n, v[p][:, n * COLS:(n + 1) * COLS], bank(front, F_QKV + 4 + n))
                if on(k):
                    copy(back, k, B_PT + 3, probT[:, 3].rearrange("p j s -> p (j s)"), bank(back, B_PT + 3))
                    for u in range(2):
                        copy(back, k, B_OT + u, oT[:, 4 * u:4 * u + 4, :].rearrange("p c s -> p (c s)"),
                             bank(back, B_OT + u))
                if on(a):
                    xmax_fill(a, 0)
                    xmax_fill(a, 1)
                if on(c):
                    dve.wait_ge(crossb.drained[0], crossb.count(c, C_XT))
                    hi = x2T_hi[:, bass.ds(c * S, S)]
                    nc.vector.tensor_copy(hi, x2T[:]).then_inc(x2_hi_ready, 1)
                    dve.wait_ge(x2_hi_ready, c + 1)
                    nc.vector.tensor_tensor(x2T_lo[:, bass.ds(c * S, S)], x2T[:], hi.bitcast(F32),
                                            ALU.subtract).then_inc(x2_split, 1)
                    filled(crossb, c, C_R)
                    nc.vector.tensor_tensor(logits[:, bass.ds(c, 1), :].rearrange("p a e -> p (a e)"),
                                            bank(crossb, C_R)[:, 0:E], rb_sb[:], ALU.add).then_inc(crossb.drained[0], 1)
                if on(a):
                    xmax_fill(a, 2)
                    xmax_fill(a, 3)
                if on(f):
                    for n in range(2):
                        copy(front, f, F_T + 2 + n, kT[p][:, 4 * n:4 * n + 4, :].rearrange("p c s -> p (c s)"),
                             bank(front, F_T + 2 + n))
                if on(a):
                    copy(crossa, a, A_PT + 1, xprobT[:, 1].rearrange("p j s -> p (j s)"), bank(crossa, A_PT + 1))
                if on(k):
                    filled(back, k, B_Y)
                    dve.wait_ge(xres_loaded[q], loads(k, q))
                    nc.vector.tensor_tensor(y1[:], bank(back, B_Y)[:, 0:D], xres[q][:], ALU.add)\
                        .then_inc(back.drained[B_Y % back.n], 1)
                    layer_norm(k, y1, st1, mv1, rstd1, x1c[q][:], x1[q][:], back, B_Y, st1_ready, mv1_ready, rstd1_ready, x1_ready)
                if on(a):
                    copy(crossa, a, A_PT + 3, xprobT[:, 3].rearrange("p j s -> p (j s)"), bank(crossa, A_PT + 3))

            slots(dve, slot)

        @block.tensor
        def _(pe):
            def free(ring, b, fill):
                wait(pe, ring.drained[fill % ring.n], ring.count(b, fill) - 1)
                return ps[:, ring.bank(fill), :]

            def evacuated(ring, b, fill):
                pe.wait_ge(ring.drained[fill % ring.n], ring.count(b, fill))

            def transpose(dst, src, n=128):
                return nc.tensor.transpose(dst, src, ident[:])

            pe.wait_ge(wqkv_loaded, 16)
            pe.wait_ge(w_loaded, 16 * len(small))
            pe.wait_ge(masks_made, 1)
            pe.wait_ge(const_ready, 4)

            def x_transpose(b, p):
                pe.wait_ge(xf_loaded[p], loads(b, p))
                dst = free(front, b, F_XT)
                transpose(dst[:, 0:S], xf[p][:]).then_inc(front.filled[0], 1)

            def qkv(b, n):
                if n == 0:
                    evacuated(front, b, F_XT)
                dst = free(front, b, F_QKV + n)
                cols = slice(n * COLS, (n + 1) * COLS)
                nc.tensor.matmul(dst, xT_hi[:], w_lo[:, cols], start=True, stop=False)
                nc.tensor.matmul(dst, xT_lo[:], w_hi[:, cols], start=False, stop=False)
                nc.tensor.matmul(dst, xT_hi[:], w_hi[:, cols], start=False, stop=True)\
                    .then_inc(front.filled[(F_QKV + n) % 2], 1)

            def qk_transpose(b, n):
                pe.wait_ge(roped, 4 * b + n + 1)
                dst = free(front, b, F_T + n)
                for j in range(4):
                    last = transpose(dst[:, j * S:(j + 1) * S],
                                     qk[:, 8 * n + 2 * j:8 * n + 2 * j + 2, :].rearrange("p h k -> p (h k)"))
                last.then_inc(front.filled[(F_T + n) % 2], 1)

            def scores(b, q, u):
                if u == 0:
                    for n in range(4):
                        evacuated(front, b, F_T + n)
                dst = [free(back, b, B_S + 2 * u + r) for r in range(2)]
                for r in range(2):
                    nc.tensor.matmul(dst[r], identb[:], causal[:].rearrange("p j s -> p (j s)"), start=True, stop=False,
                                     skip_group_check=True)
                for j in range(4):
                    for r in range(2):
                        rows = slice(64 * r, 64 * r + 64)
                        last = nc.tensor.matmul(dst[r][:, j * S:(j + 1) * S], qT[q][rows, 4 * u + j, :],
                                                kT[q][rows, 4 * u + j, :], start=False, stop=(j == 3),
                                                skip_group_check=True)
                        if j == 3:
                            last.then_inc(back.filled[(B_S + 2 * u + r) % back.n], 1)

            def prob_transpose(b, f):
                pe.wait_ge(normed, 4 * b + f + 1)
                dst = free(back, b, B_PT + f)
                for j in range(4):
                    last = transpose(dst[:, j * S:(j + 1) * S], prob[:, f, j, :])
                last.then_inc(back.filled[(B_PT + f) % back.n], 1)

            def pv(b, q, u):
                for r in range(2):
                    evacuated(back, b, B_PT + 2 * u + r)
                dst = free(back, b, B_OT + u)
                for j in range(4):
                    for r in range(2):
                        h = 2 * (4 * u + j) + r
                        last = nc.tensor.matmul(dst[64 * r:64 * r + 64, j * S:(j + 1) * S],
                                                v[q][:, h * DK:(h + 1) * DK], probT[:, 2 * u + r, j, :],
                                                start=True, stop=True)
                last.then_inc(back.filled[(B_OT + u) % back.n], 1)

            def out_proj(b):
                for u in range(2):
                    evacuated(back, b, B_OT + u)
                dst = free(back, b, B_Y)
                for c in range(CH):
                    last = nc.tensor.matmul(dst[:, 0:D], oT[:, c, :], wo_sb[:, c, :], start=(c == 0), stop=(c == CH - 1))
                last.then_inc(back.filled[B_Y % back.n], 1)

            def xscores(b, u):
                if u == 0:
                    evacuated(crossa, b, A_QT)
                    evacuated(crossa, b, A_KT)
                dst = [free(crossa, b, A_S + 2 * u + r) for r in range(2)]
                for c in range(GRP):
                    for r in range(2):
                        g = 2 * u + r
                        rows = slice(32 * g, 32 * g + XK + 1)
                        last = nc.tensor.matmul(dst[r][:, c * S:(c + 1) * S], xqT[rows, c, :], xkT[rows, :],
                                                start=True, stop=True)
                        if c == GRP - 1:
                            last.then_inc(crossa.filled[(A_S + g) % 2], 1)

            def xprob_transpose(b, g):
                pe.wait_ge(xexp, 4 * b + g + 1)
                dst = free(crossa, b, A_PT + g)
                for c in range(GRP):
                    last = transpose(dst[:, c * S:(c + 1) * S], xprob[:, g, c, :])
                last.then_inc(crossa.filled[(A_PT + g) % 2], 1)

            def slot(s, p, f, k, a, c):
                q = 1 - p
                if on(f):
                    x_transpose(f, p)
                if on(k):
                    scores(k, q, 0)
                if on(c):
                    evacuated(crossa, c, A_OT)
                    dst = free(crossb, c, C_O)
                    for j in range(GRP):
                        last = transpose(dst[:, j * S:(j + 1) * S], xoT[q][:, j, :])
                    last.then_inc(crossb.filled[0], 1)
                if on(k):
                    scores(k, q, 1)
                if on(a):
                    pe.wait_ge(x1_ready, a + 1)
                    pe.wait_ge(cx_loaded[p], loads(a, p))
                    dst = free(crossa, a, A_T)
                    transpose(dst[:, 0:S], x1[p][:])
                    transpose(dst[:, S:2 * S], cx[p][:]).then_inc(crossa.filled[0], 1)
                if on(f):
                    if isinstance(s, int) and s == 0:
                        pe.wait_ge(w_lo_ready, 2)
                    qkv(f, 0)
                    qkv(f, 1)
                if on(c):
                    evacuated(crossb, c, C_O)
                    dst = free(crossb, c, C_T)
                    transpose(dst[:, 0:S], xo[:]).then_inc(crossb.filled[0], 1)
                if on(f):
                    qkv(f, 2)
                    qkv(f, 3)
                if on(a):
                    evacuated(crossa, a, A_T)
                    dst = free(crossa, a, A_QKV)
                    nc.tensor.matmul(dst[:, 0:128], xcT[:, 0, :], xwq_sb[:], start=True, stop=True)
                    nc.tensor.matmul(dst[:, 128:192], xcT[:, 1, :], xwkv_sb[:], start=True, stop=True)\
                        .then_inc(crossa.filled[A_QKV % 2], 1)
                if on(k):
                    prob_transpose(k, 0)
                    prob_transpose(k, 1)
                if on(c):
                    evacuated(crossb, c, C_T)
                    dst = free(crossb, c, C_Y)
                    nc.tensor.matmul(dst[:, 0:D], xonT[:], xwo_sb[:], start=True, stop=True).then_inc(crossb.filled[0], 1)
                if on(f):
                    qkv(f, 4)
                    qkv(f, 5)
                if on(a):
                    pe.wait_ge(xpads_ready, 4 * (a + 1))
                    dst = free(crossa, a, A_QT)
                    for j in range(GRP):
                        last = transpose(dst[:, j * S:(j + 1) * S], xq_pad[:, j].rearrange("p g r -> p (g r)"))
                    last.then_inc(crossa.filled[A_QT % 2], 1)
                    dst = free(crossa, a, A_KT)
                    transpose(dst[:, 0:S], xk_pad[:].rearrange("p g r -> p (g r)")).then_inc(crossa.filled[A_KT % 2], 1)
                if on(k):
                    prob_transpose(k, 2)
                    prob_transpose(k, 3)
                if on(c):
                    pe.wait_ge(x2_ready, c + 1)
                    transpose(ps[:, 7, 0:S], x2[:]).then_inc(crossb.filled[0], 1)
                if on(k):
                    pv(k, q, 0)
                    pv(k, q, 1)
                if on(a):
                    xscores(a, 0)
                if on(f):
                    qk_transpose(f, 0)
                    qk_transpose(f, 1)
                if on(c):
                    evacuated(crossb, c, C_XT)
                    nc.tensor.matmul(ps[:, 7, 0:E], x2T[:], rw_sb[:], start=True, stop=True).then_inc(crossb.filled[0], 1)
                if on(a):
                    xscores(a, 1)
                if on(f):
                    qk_transpose(f, 2)
                    qk_transpose(f, 3)
                if on(a):
                    xprob_transpose(a, 0)
                    xprob_transpose(a, 1)
                if on(k):
                    out_proj(k)
                if on(a):
                    xprob_transpose(a, 2)
                    xprob_transpose(a, 3)
                    for g in range(4):
                        evacuated(crossa, a, A_PT + g)
                    dst = free(crossa, a, A_OT)
                    for g in range(XG):
                        last = nc.tensor.matmul(dst[32 * g:32 * g + 32, :], xv[p][:, g, :],
                                                xprobT[:, g].rearrange("p c s -> p (c s)"), start=True, stop=True,
                                                skip_group_check=True)
                    last.then_inc(crossa.filled[A_OT % 2], 1)

            slots(pe, slot)


def ffn_phase(nc, sem, ps, x2_all, x2T_hi, x2T_lo, logits, ident, mhalf, eps, scratch, temp, eidx, fwg, fwp, fwo, out):
    NF = E * FF // 128
    with ExitStack() as phase:
        def sb(name, shape, dt=F32):
            return phase.enter_context(nc.sbuf_tensor(name, shape, dt))

        stage = [sb(f"fstage{i}", [128, E * FF]) for i in range(2)]
        w_hi = [sb(f"fw_hi{i}", [128, E * FF], F32R) for i in range(2)]
        w_lo = [sb(f"fw_lo{i}", [128, E * FF], F32R) for i in range(2)]
        wo_sb = sb("fwo_sb", [128, NF, D])
        temp_sb = sb("temp_sb", [128, 1])
        eidx_sb = sb("eidx_sb", [128, E])
        rtemp = sb("rtemp", [128, 2])
        la = sb("la", [128, B, E])
        laT = sb("laT", [128, 2, S])
        dif = sb("dif", [128, B, E])
        ex = sb("ex", [128, B, E])
        exT = sb("exT", [128, 2, S])
        rmax = sb("rmax", [128, B])
        rsum = sb("rsum", [128, B])
        rlog = sb("rlog", [128, B])
        cmax = sb("cmax", [128, 2])
        csum = sb("csum", [128, 2])
        clog = sb("clog", [128, 2])
        gates = sb("gates", [128, B, E])
        cand = sb("cand", [128, B, E])
        one = [sb(f"one{i}", [128, B, E]) for i in range(2)]
        top = [sb(f"top{i}", [128, B]) for i in range(2)]
        low = sb("low", [128, B])
        wts = sb("wts", [128, B, E])
        gs = [sb(f"gs{i}", [128, FB * S]) for i in range(2)]
        h = [sb(f"h{i}", [128, FB * S]) for i in range(4)]
        part = [sb(f"part{i}", [128, FB, D]) for i in range(2)]
        acc = sb("acc", [128, FB, D])
        st3 = sb("st3", [128, FB, 6])
        mv3 = sb("mv3", [128, FB, 2])
        ve3 = sb("ve3", [128, FB])
        rstd3 = sb("rstd3", [128, FB])
        yo = sb("yo", [128, FB, D])

        up = Ring(sem, "up", [0, 1, 2, 3], 2 * NF)
        down = Ring(sem, "down", [4, 5], E)
        f_loaded = sem("f_loaded")
        fc_loaded = sem("fc_loaded")
        fo_loaded = sem("fo_loaded")
        f_hi = sem("f_hi")
        f_lo = sem("f_lo")
        sk_dve = sem("sk_dve")
        sk_act = sem("sk_act")
        sk_scaled = sem("sk_scaled")
        sk_pe = sem("sk_pe")
        acc_done = sem("acc_done")
        st3_ready = sem("st3_ready")
        mv3_ready = sem("mv3_ready")
        ve3_ready = sem("ve3_ready")
        rstd3_ready = sem("rstd3_ready")
        yo_ready = sem("yo_ready")
        stored = sem("stored")

        there, again = ps[:, 6, 0:2 * S], ps[:, 7, 0:2 * S]
        flat = lambda t: t[:].rearrange("p b e -> p (b e)")
        over_e = lambda t: t[:, :, None].broadcast_to([128, B, E])

        def groups(eng, group):
            group(0)
            with eng.Fori(1, B // FB) as g:
                group(g)

        DS, AS, PS = 6, 4, 2

        block = phase.enter_context(nc.Block())

        @block.sync
        def _(sp):
            sp.dma_start(temp_sb[:], temp).then_inc(fc_loaded, 16)
            sp.dma_start(eidx_sb[:], eidx).then_inc(fc_loaded, 16)
            sp.dma_start(stage[0][:], fwg).then_inc(f_loaded, 16)
            sp.dma_start(stage[1][:], fwp).then_inc(f_loaded, 16)
            sp.dma_start(wo_sb[:], fwo.rearrange("(n p) d -> p n d", p=128)).then_inc(fo_loaded, 16)

            def group(g):
                sp.wait_ge(yo_ready, FB * (g + 1))
                sp.dma_start(out[bass.ds(g * FB, FB), :, :].rearrange("a s d -> s a d"), yo[:]).then_inc(stored, 16)

            groups(sp, group)
            sp.wait_ge(stored, 16 * (B // FB))

        @block.gpsimd
        def _(pool):
            for i in range(2):
                pool.wait_ge(f_hi, i + 1)
                nc.gpsimd.tensor_tensor(w_lo[i][:], stage[i][:], w_hi[i][:].bitcast(F32), ALU.subtract).then_inc(f_lo, 1)

            def group(g):
                for e in range(E):
                    pool.wait_ge(down.drained[e % 2], down.count(g, e))
                    if e == 0:
                        wait(pool, yo_ready, FB * g)
                        own = x2_all[:, bass.ds(g * FB, FB), :]
                        nc.gpsimd.tensor_tensor(acc[:], own, own, ALU.add).then_inc(acc_done, 1)
                    pool.wait_ge(acc_done, (E + 1) * g + e + 1)
                    nc.gpsimd.tensor_tensor(acc[:], acc[:], part[e % 2][:], ALU.add).then_inc(acc_done, 1)
                pool.wait_ge(mv3_ready, FB * (g + 1))
                nc.gpsimd.tensor_tensor(ve3[:], mv3[:, :, 1], eps[:], ALU.add).then_inc(ve3_ready, 1)
                pool.wait_ge(ve3_ready, g + 1)
                nc.gpsimd.tensor_tensor(rstd3[:], ve3[:], mhalf[:], ALU.pow).then_inc(rstd3_ready, 1)

            groups(pool, group)

        @block.scalar
        def _(act):
            for i in range(2):
                act.wait_ge(f_loaded, 32)
                nc.scalar.activation(w_hi[i][:], stage[i][:], ACT.Copy).then_inc(f_hi, 1)
            for it in range(SINKHORN_ITERS):
                act.wait_ge(sk_dve, 2 + DS * it + 2)
                nc.scalar.activation(flat(ex), flat(dif), ACT.Exp).then_inc(sk_act, 1)
                act.wait_ge(sk_dve, 2 + DS * it + 3)
                nc.scalar.activation(rlog[:], rsum[:], ACT.Ln).then_inc(sk_act, 1)
                act.wait_ge(sk_dve, 2 + DS * it + 5)
                for j in range(2):
                    last = nc.scalar.activation(exT[:, j, :], there[:, j * S:(j + 1) * S], ACT.Exp, bias=cmax[:, j:j + 1],
                                                accum_out=csum[:, j:j + 1])
                last.then_inc(sk_act, 1)
                act.wait_ge(sk_act, AS * it + 3)
                nc.scalar.activation(clog[:], csum[:], ACT.Ln).then_inc(sk_act, 1)
            act.wait_ge(sk_pe, PS * SINKHORN_ITERS)
            nc.scalar.activation(flat(ex), again, ACT.Exp).then_inc(sk_act, 1)

            def group(g):
                for n in range(NF):
                    act.wait_ge(up.filled[(2 * n) % 4], up.count(g, 2 * n))
                    wait(act, up.drained[(2 * n + 1) % 4], up.count(g, 2 * n + 1) - 1)
                    nc.scalar.activation(gs[n % 2][:], ps[:, up.bank(2 * n), :], ACT.Relu)\
                        .then_inc(up.drained[(2 * n) % 4], 1)

            groups(act, group)

        @block.vector
        def _(dve):
            steps = [0]

            def link(ins):
                steps[0] += 1
                ins.then_inc(sk_dve, 1)
                dve.wait_ge(sk_dve, steps[0])

            dve.wait_ge(fc_loaded, 32)
            link(nc.vector.tensor_scalar(rtemp[:, 0:1], temp_sb[:], 0.1, None, ALU.max))
            link(nc.vector.reciprocal(rtemp[:, 1:2], rtemp[:, 0:1]))
            sc_step = nc.vector.tensor_scalar(flat(la), flat(logits), rtemp[:, 1:2], None, ALU.mult)
            for it in range(SINKHORN_ITERS):
                if it == 0:
                    sc_step.then_inc(sk_scaled, 1)
                    dve.wait_ge(sk_scaled, 1)
                    src = la[:]
                else:
                    dve.wait_ge(sk_pe, PS * it)
                    src = again.rearrange("p (b e) -> p b e", b=B)
                link(nc.vector.tensor_reduce(rmax[:], src, AX_X, ALU.max))
                link(nc.vector.tensor_tensor(dif[:], src, over_e(rmax), ALU.subtract))
                dve.wait_ge(sk_act, AS * it + 1)
                link(nc.vector.tensor_reduce(rsum[:], ex[:], AX_X, ALU.add))
                dve.wait_ge(sk_act, AS * it + 2)
                link(nc.vector.tensor_tensor(la[:], dif[:], over_e(rlog), ALU.subtract))
                dve.wait_ge(sk_pe, PS * it + 1)
                link(nc.vector.tensor_reduce(cmax[:], there.rearrange("p (j s) -> p j s", j=2), AX_X, ALU.max, negate=True))
                dve.wait_ge(sk_act, AS * it + 4)
                for j in range(2):
                    last = nc.vector.tensor_scalar(laT[:, j, :], there[:, j * S:(j + 1) * S], cmax[:, j:j + 1],
                                                   clog[:, j:j + 1], ALU.add, ALU.subtract)
                link(last)
            dve.wait_ge(sk_act, AS * SINKHORN_ITERS + 1)
            link(nc.vector.tensor_reduce(rsum[:], ex[:], AX_X, ALU.add))
            link(nc.vector.tensor_scalar(rlog[:], rsum[:], 1e-8, None, ALU.add))
            link(nc.vector.reciprocal(rmax[:], rlog[:]))
            link(nc.vector.tensor_tensor(gates[:], ex[:], over_e(rmax), ALU.mult))
            src = gates
            idx = eidx_sb[:, None, :].broadcast_to([128, B, E])
            for i in range(2):
                link(nc.vector.tensor_reduce(top[i][:], src[:], AX_X, ALU.max))
                link(nc.vector.tensor_tensor(cand[:], src[:], over_e(top[i]), ALU.is_equal))
                link(nc.vector.tensor_tensor(cand[:], cand[:], idx, ALU.mult))
                link(nc.vector.tensor_reduce(low[:], cand[:], AX_X, ALU.min))
                link(nc.vector.tensor_tensor(one[i][:], cand[:], over_e(low), ALU.is_equal))
                if i == 0:
                    link(nc.vector.scalar_tensor_tensor(flat(dif), flat(one[0]), -4.0, flat(gates), ALU.mult, ALU.add))
                    src = dif
            link(nc.vector.scalar_tensor_tensor(rsum[:], top[0][:], 1e-8, top[1][:], ALU.add, ALU.add))
            link(nc.vector.reciprocal(rlog[:], rsum[:]))
            link(nc.vector.tensor_tensor(cand[:], one[0][:], one[1][:], ALU.add))
            link(nc.vector.tensor_tensor(ex[:], cand[:], gates[:], ALU.mult))
            link(nc.vector.tensor_tensor(wts[:], ex[:], over_e(rlog), ALU.mult))

            def hidden(g, n):
                dve.wait_ge(up.filled[(2 * n + 1) % 4], up.count(g, 2 * n + 1))
                dve.wait_ge(up.drained[(2 * n) % 4], up.count(g, 2 * n))
                if n % 2 == 0:
                    wait(dve, down.filled[(n // 2) % 2], down.count(g, n // 2) - 1)
                nc.vector.tensor_tensor(h[n % 4][:], ps[:, up.bank(2 * n + 1), :], gs[n % 2][:], ALU.mult)\
                    .then_inc(up.drained[(2 * n + 1) % 4], 1)

            def combine(g, e):
                dve.wait_ge(down.filled[e % 2], down.count(g, e))
                if not isinstance(g, int) or e >= 2:
                    wait(dve, acc_done, (E + 1) * g + e)
                nc.vector.tensor_tensor(part[e % 2][:], ps[:, down.bank(e), :].rearrange("p (b d) -> p b d", b=FB),
                                        wts[:, bass.ds(g * FB, FB), e:e + 1].broadcast_to([128, FB, D]), ALU.mult)\
                    .then_inc(down.drained[e % 2], 1)

            def group(g):
                for e in range(E):
                    hidden(g, 2 * e)
                    hidden(g, 2 * e + 1)
                    if e:
                        combine(g, e - 1)
                combine(g, E - 1)
                dve.wait_ge(acc_done, (E + 1) * (g + 1))
                for b in range(FB):
                    nc.vector.bn_stats(st3[:, b, :], acc[:, b, :]).then_inc(st3_ready, 1)
                dve.wait_ge(st3_ready, FB * (g + 1))
                nc.vector.memset(scratch[:], 0.0)
                for b in range(FB):
                    nc.vector.bn_aggr(mv3[:, b, :], st3[:, b, :]).then_inc(mv3_ready, 1)
                dve.wait_ge(rstd3_ready, g + 1)
                wait(dve, stored, 16 * g)
                for b in range(FB):
                    nc.vector.tensor_scalar(yo[:, b, :], acc[:, b, :], mv3[:, b, 0:1], rstd3[:, b:b + 1],
                                            ALU.subtract, ALU.mult).then_inc(yo_ready, 1)

            groups(dve, group)

        @block.tensor
        def _(pe):
            for it in range(SINKHORN_ITERS):
                pe.wait_ge(sk_dve, 2 + DS * it + 4)
                for j in range(2):
                    last = nc.tensor.transpose(there[:, j * S:(j + 1) * S], flat(la)[:, j * 128:(j + 1) * 128], ident[:])
                last.then_inc(sk_pe, 1)
                pe.wait_ge(sk_dve, 2 + DS * it + 6)
                for j in range(2):
                    last = nc.tensor.transpose(again[:, j * 128:(j + 1) * 128], laT[:, j, :], ident[:])
                last.then_inc(sk_pe, 1)
            pe.wait_ge(f_lo, 2)
            pe.wait_ge(fo_loaded, 16)

            def expert_up(g, n):
                cols = slice(n * 128, (n + 1) * 128)
                hi, lo = x2T_hi[:, bass.ds(g * FB * S, FB * S)], x2T_lo[:, bass.ds(g * FB * S, FB * S)]
                for i in range(2):
                    fill = 2 * n + i
                    wait(pe, up.drained[fill % 4], up.count(g, fill) - 1)
                    dst = ps[:, up.bank(fill), :]
                    nc.tensor.matmul(dst, w_lo[i][:, cols], hi, start=True, stop=False)
                    nc.tensor.matmul(dst, w_hi[i][:, cols], lo, start=False, stop=False)
                    nc.tensor.matmul(dst, w_hi[i][:, cols], hi, start=False, stop=True).then_inc(up.filled[fill % 4], 1)

            def expert_down(g, e):
                for n in (2 * e, 2 * e + 1):
                    pe.wait_ge(up.drained[(2 * n + 1) % 4], up.count(g, 2 * n + 1))
                wait(pe, down.drained[e % 2], down.count(g, e) - 1)
                for b in range(FB):
                    for n in (2 * e, 2 * e + 1):
                        last = nc.tensor.matmul(ps[:, down.bank(e), b * D:(b + 1) * D], h[n % 4][:, b * S:(b + 1) * S],
                                                wo_sb[:, n, :], start=(n % 2 == 0), stop=(n % 2 == 1))
                last.then_inc(down.filled[e % 2], 1)

            def group(g):
                for e in range(E):
                    expert_up(g, 2 * e)
                    expert_up(g, 2 * e + 1)
                    if e:
                        expert_down(g, e - 1)
                expert_down(g, E - 1)

            groups(pe, group)


def _tables():
    f = np.float32
    tok = np.arange(S, dtype=f)
    inv = f(1.0) / f(6000.0) ** (np.arange(0, ROPE, 2, dtype=f) / f(ROPE))
    ang = np.outer(tok, inv).astype(f)
    cosq = np.concatenate([np.cos(ang)] * 2, axis=1)
    sinq = np.concatenate([-np.sin(ang), np.sin(ang)], axis=1)
    theta = f(10000.0) ** (-np.arange(0, XK, 2, dtype=f) / f(XK))
    xang = (tok[:, None] * theta[None, :]).astype(f)
    xc = np.concatenate([np.cos(xang)] * 2, axis=1)
    xs = np.concatenate([-np.sin(xang), np.sin(xang)], axis=1)
    scale = f(1.0) / np.sqrt(f(XK))
    xcos = np.concatenate([np.tile(xc * scale, (1, XH)), np.tile(xc, (1, XG))], axis=1)
    xsin = np.concatenate([np.tile(xs * scale, (1, XH)), np.tile(xs, (1, XG))], axis=1)
    causal = np.where(np.arange(S)[None, :] > np.arange(S)[:, None], f(CAUSAL), f(0.0))
    eidx = np.tile(np.arange(E, dtype=f) - f(E), (128, 1))
    return [a.astype(f) for a in (cosq, sinq, xcos, xsin, np.eye(128), causal, eidx)]


def kernel(**inputs):
    import concourse.bacc as bacc
    from concourse.bass_utils import run_bass_kernel_spmd

    a = {k: np.asarray(v) for k, v in inputs.items()}
    cosq, sinq, xcos, xsin, ident, causal, eidx = _tables()
    arrays = {
        "x": a["x"], "ctx": a["ctx_1024"],
        "qmask": a["mask_BxS2_bf1"].T, "kpad": a["mask_BxS2_bk0"].T,
        "cosq": cosq, "sinq": sinq, "xcos": xcos, "xsin": xsin, "ident": ident, "causal": causal,
        "wqkv": a["L0_attn_W_qkv"].reshape(QKV, D).T, "wo": a["L0_attn_W_o"].T,
        "xwq": a["L0_xattn_w_q"], "xwkv": np.concatenate([a["L0_xattn_w_k"], a["L0_xattn_w_v"]], axis=1),
        "xwo": a["L0_xattn_w_out"],
        "rw": a["L0_ffn_router_w"].T, "rb": np.broadcast_to(a["L0_ffn_router_b"], (128, E)),
        "temp": np.broadcast_to(a["L0_ffn_temperature"], (128, 1)), "eidx": eidx,
        "fwg": a["L0_ffn_wg"].transpose(1, 0, 2).reshape(D, E * FF),
        "fwp": a["L0_ffn_wp"].transpose(1, 0, 2).reshape(D, E * FF),
        "fwo": a["L0_ffn_wo"].reshape(E * FF, D),
    }
    arrays = {k: np.ascontiguousarray(v) for k, v in arrays.items()}
    nc = bacc.Bacc("TRN2", target_bir_lowering=False, num_devices=1)
    args = [nc.dram_tensor(f"in_{k}", v.shape, mybir.dt.from_np(v.dtype), kind="ExternalInput").ap() for k, v in arrays.items()]
    args.append(nc.dram_tensor("out_y", (B, S, D), F32, kind="ExternalOutput").ap())
    decoder_layer(nc, *args)
    r = run_bass_kernel_spmd(nc, [{f"in_{k}": v for k, v in arrays.items()}], core_ids=[0])
    return r.results[0]["out_y"]
```

```python
from contextlib import ExitStack

import numpy as np
import concourse.bass as bass
from concourse import mybir

F32 = mybir.dt.float32
F32R = mybir.dt.float32r
BF16 = mybir.dt.bfloat16
U8 = mybir.dt.uint8
ALU = mybir.AluOpType
ACT = mybir.ActivationFunctionType
AX_X = mybir.AxisListType.X

B, S, D = 32, 128, 128
H, DK = 16, 64
ROPE = DK // 2
XH, XG, XK = 16, 4, 8
GRP = XH // XG
E, FF = 8, 256
QKV = 3 * H * DK
COLS = 512
CH = H * DK // D
EPS = 1e-5
CAUSAL = -1.0e30
BIG = float(2.0 ** 127)
FB = 4
SINKHORN_ITERS = 3


class Ring:

    def __init__(self, sem, name, banks, fills):
        self.banks = banks
        self.n = len(banks)
        self.per = [len(range(k, fills, self.n)) for k in range(self.n)]
        self.filled = [sem(f"{name}_filled{k}") for k in range(self.n)]
        self.drained = [sem(f"{name}_drained{k}") for k in range(self.n)]

    def bank(self, fill):
        return self.banks[fill % self.n]

    def count(self, b, fill):
        return b * self.per[fill % self.n] + fill // self.n + 1


class SlotRing:

    def __init__(self, sem, order):
        self.order = order
        self.at = {name: i for i, name in enumerate(order)}
        self.filled = [sem(f"bank_filled{k}") for k in range(8)]
        self.drained = [sem(f"bank_drained{k}") for k in range(8)]
        self.first_full = 3

    def bank(self, name):
        return self.at[name] % 8

    def count(self, s, name):
        i = self.at[name]
        if not isinstance(s, int):
            per = len(range(i % 8, len(self.order), 8))
            return s * per + (self.count(self.first_full, name) - per * self.first_full)
        total = 0
        for slot in range(s + 1):
            for j in range(i % 8, len(self.order) if slot < s else i + 1, 8):
                if 0 <= slot - STAGE[self.order[j][0]] < B:
                    total += 1
        return total


STAGE = {"f": 0, "k": 1, "a": 2, "c": 3}


def wait(eng, sem, value):
    if isinstance(value, int) and value <= 0:
        return
    eng.wait_ge(sem, value)


def decoder_layer(nc, x, ctx, qmask, kpad, cosq, sinq, xcos, xsin, ident_d, causal_d, gsel_d, wqkv, wo, xwq, xwkv, xwo,
                  rw, rb, temp, eidx, fwg, fwp, fwo, out):
    with ExitStack() as whole:
        def sem(name):
            return whole.enter_context(nc.semaphore(name))

        def keep(name, shape, dt=F32):
            return whole.enter_context(nc.sbuf_tensor(name, shape, dt))

        ps = whole.enter_context(nc.psum_tensor("ps", [128, 8, COLS], F32))
        x2_all = keep("x2_all", [128, B, D])
        x2T_hi = keep("x2T_hi", [128, B * S], F32R)
        x2T_lo = keep("x2T_lo", [128, B * S], F32R)
        logits = keep("logits", [128, B, E])
        ident = keep("ident", [128, 128])
        mhalf = keep("mhalf", [128, FB])
        scratch = keep("scratch", [128, 1])
        eps = keep("eps", [128, FB])

        attention_phase(nc, sem, ps, x2_all, x2T_hi, x2T_lo, logits, ident, mhalf, eps, scratch, x, ctx, qmask, kpad, cosq, sinq,
                        xcos, xsin, ident_d, causal_d, gsel_d, wqkv, wo, xwq, xwkv, xwo, rw, rb)
        ffn_phase(nc, sem, ps, x2_all, x2T_hi, x2T_lo, logits, ident, mhalf, eps, scratch, temp, eidx, fwg, fwp, fwo, out)


def attention_phase(nc, sem, ps, x2_all, x2T_hi, x2T_lo, logits, ident, mhalf, eps, scratch, x, ctx, qmask, kpad, cosq, sinq,
                    xcos, xsin, ident_d, causal_d, gsel_d, wqkv, wo, xwq, xwkv, xwo, rw, rb):
    with ExitStack() as phase:
        def sb(name, shape, dt=F32):
            return phase.enter_context(nc.sbuf_tensor(name, shape, dt))

        w_hi = sb("w_hi", [128, QKV], F32R)
        w_lo = sb("w_lo", [128, QKV], F32R)
        wo_sb = sb("wo_sb", [128, CH, D])
        xwq_sb = sb("xwq_sb", [128, XH * XK])
        xwkv_sb = sb("xwkv_sb", [128, 2 * XG * XK])
        xwo_sb = sb("xwo_sb", [128, D])
        rw_sb = sb("rw_sb", [128, E])
        rb_sb = sb("rb_sb", [128, E])
        identb = sb("identb", [128, 128], BF16)
        causal = sb("causal", [128, 4, 128], BF16)
        causal_f = sb("causal_f", [128, 128])
        gsel = sb("gsel", [128, XG])
        cos_sb = sb("cos_sb", [128, ROPE])
        sin_sb = sb("sin_sb", [128, ROPE])
        xcos_sb = sb("xcos_sb", [128, XH + XG, XK])
        xsin_sb = sb("xsin_sb", [128, XH + XG, XK])
        qm_u8 = sb("qm_u8", [128, B], U8)
        kp_u8 = sb("kp_u8", [128, B], U8)
        qm_all = sb("qm_all", [128, B])
        kb_all = sb("kb_all", [128, B])
        xf = [sb(f"xf{p}", [128, D]) for p in range(2)]
        xT_hi = sb("xT_hi", [128, S], F32R)
        xT_lo = sb("xT_lo", [128, S], F32R)
        qk = sb("qk", [128, 2 * H, DK])
        qk_sin = sb("qk_sin", [128, 2 * H, ROPE])
        qk_cos = sb("qk_cos", [128, 2 * H, ROPE])
        qT = [sb(f"qT{p}", [128, CH, S]) for p in range(2)]
        kT = [sb(f"kT{p}", [128, CH, S]) for p in range(2)]
        v = [sb(f"v{p}", [128, H * DK]) for p in range(2)]
        prob = sb("prob", [128, 4, 4, S])
        probT = sb("probT", [128, 4, 4, S])
        negmax = sb("negmax", [128, 4, 4])
        sums = sb("sums", [128, 4, 4])
        recip = sb("recip", [128, 4, 4])
        oT = sb("oT", [128, CH, S])
        xres = [sb(f"xres{p}", [128, D]) for p in range(2)]
        y1 = sb("y1", [128, D])
        st1 = sb("st1", [128, 6])
        mv1 = sb("mv1", [128, 2])
        ve1 = sb("ve1", [128, 1])
        rstd1 = sb("rstd1", [128, 1])
        x1 = sb("x1", [128, D])
        x1c = [sb(f"x1c{p}", [128, D]) for p in range(2)]
        cx = [sb(f"cx{p}", [128, D]) for p in range(2)]
        xcT = sb("xcT", [128, 2, S])
        xt1 = sb("xt1", [128, XH + XG, XK])
        xt2 = sb("xt2", [128, XH + XG, XK])
        xr = sb("xr", [128, XH + XG, XK])
        qm = sb("qm", [128, 1])
        xq_pad = sb("xq_pad", [128, GRP, 128], F32R)
        xk_pad = sb("xk_pad", [128, 128], F32R)
        xqT = sb("xqT", [128, GRP, S], F32R)
        xkT = sb("xkT", [128, XG, S], F32R)
        xv = [sb(f"xv{p}", [128, XG, 32]) for p in range(2)]
        xmax = sb("xmax", [128, GRP, XG])
        xprob = sb("xprob", [128, GRP, XG, S])
        xprobT = sb("xprobT", [128, GRP, XG, S])
        xoT = sb("xoT", [128, GRP, S])
        xrec = sb("xrec", [128, GRP, XG])
        xo = sb("xo", [128, XH * XK])
        xonT = sb("xonT", [128, S])
        y2 = sb("y2", [128, D])
        st2 = sb("st2", [128, 6])
        mv2 = sb("mv2", [128, 2])
        ve2 = sb("ve2", [128, 1])
        rstd2 = sb("rstd2", [128, 1])
        x2 = sb("x2", [128, D])
        x2T = sb("x2T", [128, S])

        xq_parts = xq_pad[:].rearrange("p c (g r) -> p (c g) r", g=XG)[:, :, 0:3 * (XK + 1)].rearrange("p h (a k) -> p h a k", a=3)
        xk_parts = xk_pad[:].rearrange("p (g r) -> p g r", g=XG)[:, :, 0:3 * (XK + 1)].rearrange("p g (a k) -> p g a k", a=3)

        ring = SlotRing(sem, [
            "c.PT0", "c.PT1", "k.S0", "k.S1", "f.XT", "a.T", "c.PT2", "c.PT3",
            "k.S2", "k.S3", "c.OT", "a.QKV", "k.PT0", "f.Q0", "f.Q1", "c.O",
            "f.Q2", "f.Q3", "k.PT1", "c.T", "f.Q4", "k.PT2", "a.QT", "a.KT",
            "c.Y", "k.PT3", "k.OT0", "a.S0", "f.T0", "f.T1", "a.S1", "k.OT1",
            "f.Q5", "a.S2", "f.T2", "c.XT", "k.Y", "a.S3", "c.R", "f.T3"])

        w_loaded = sem("w_loaded")
        wqkv_loaded = sem("wqkv_loaded")
        const_ready = sem("const_ready")
        masks_made = sem("masks_made")
        w_hi_ready = sem("w_hi_ready")
        w_lo_ready = sem("w_lo_ready")
        xf_loaded = [sem(f"xf_loaded{p}") for p in range(2)]
        xres_loaded = [sem(f"xres_loaded{p}") for p in range(2)]
        cx_loaded = [sem(f"cx_loaded{p}") for p in range(2)]
        x_hi_ready = sem("x_hi_ready")
        sin_done = sem("sin_done")
        cos_done = sem("cos_done")
        roped = sem("roped")
        maxed = sem("maxed")
        summed = sem("summed")
        normed = sem("normed")
        st1_ready = sem("st1_ready")
        mv1_ready = sem("mv1_ready")
        ve1_ready = sem("ve1_ready")
        rstd1_ready = sem("rstd1_ready")
        x1_ready = sem("x1_ready")
        xt_ready = sem("xt_ready")
        xr_ready = sem("xr_ready")
        xhi_ready = sem("xhi_ready")
        xlo_ready = sem("xlo_ready")
        xmaxed = sem("xmaxed")
        xrec_ready = sem("xrec_ready")
        st2_ready = sem("st2_ready")
        mv2_ready = sem("mv2_ready")
        ve2_ready = sem("ve2_ready")
        rstd2_ready = sem("rstd2_ready")
        x2_ready = sem("x2_ready")
        x2_hi_ready = sem("x2_hi_ready")
        x2_split = sem("x2_split")

        small = [(wo_sb[:], wo.rearrange("(c p) n -> p c n", p=128)), (xwq_sb[:], xwq), (xwkv_sb[:], xwkv),
                 (xwo_sb[:], xwo), (rw_sb[:], rw), (rb_sb[:], rb), (cos_sb[:], cosq), (sin_sb[:], sinq),
                 (xcos_sb[:].rearrange("p h k -> p (h k)"), xcos), (xsin_sb[:].rearrange("p h k -> p (h k)"), xsin),
                 (qm_u8[:], qmask), (kp_u8[:], kpad), (causal_f[:], causal_d), (gsel[:], gsel_d)]
        stage = [qk[:].rearrange("p h k -> p (h k)")[:, 0:QKV // 2], prob[:].rearrange("p a b c -> p (a b c)")[:, 0:QKV // 2]]

        def slots(eng, slot):
            for s in range(4):
                slot(s, s % 2, s, s - 1, s - 2, s - 3)
            with eng.Fori(2, B // 2) as turn:
                for p in range(2):
                    s = 2 * turn + p
                    slot(s, p, s, s - 1, s - 2, s - 3)
            for s in range(B, B + 3):
                slot(s, s % 2, s, s - 1, s - 2, s - 3)

        def loads(b, parity):
            return 8 * b + 16 - 8 * parity

        def on(b):
            return not isinstance(b, int) or 0 <= b < B

        def bank(name, n=COLS):
            return ps[:, ring.bank(name), 0:n]

        def filled(eng, s, name):
            eng.wait_ge(ring.filled[ring.bank(name)], ring.count(s, name))

        def drained(eng, s, name):
            eng.wait_ge(ring.drained[ring.bank(name)], ring.count(s, name))

        block = phase.enter_context(nc.Block())

        @block.sync
        def _(sp):
            sp.dma_start(ident[:], ident_d).then_inc(wqkv_loaded, 16)
            for half in range(2):
                sp.dma_start(stage[half], wqkv[:, half * QKV // 2:(half + 1) * QKV // 2]).then_inc(wqkv_loaded, 16)

            def slot(s, p, f, k, a, c):
                q = 1 - p
                if on(f):
                    wait(sp, x_hi_ready, f - 1)
                    sp.dma_start(xf[p][:], x[bass.ds(f, 1), :, :].rearrange("a s d -> s (a d)")).then_inc(xf_loaded[p], 16)
                if isinstance(s, int) and s == 0:
                    for dst, src in small:
                        sp.dma_start(dst, src).then_inc(w_loaded, 16)
                if on(k):
                    wait(sp, st1_ready, k - 1)
                    sp.dma_start(xres[q][:], x[bass.ds(k, 1), :, :].rearrange("a s d -> s (a d)")).then_inc(xres_loaded[q], 16)
                    wait(sp, xt_ready, k - 1)
                    sp.dma_start(cx[q][:], ctx[bass.ds(k, 1), :, :].rearrange("a s d -> s (a d)")).then_inc(cx_loaded[q], 16)

            slots(sp, slot)

        @block.gpsimd
        def _(pool):
            nc.gpsimd.memset(mhalf[:], -0.5)
            nc.gpsimd.memset(eps[:], EPS)
            nc.gpsimd.memset(xq_pad[:].bitcast(F32), 0.0)
            nc.gpsimd.memset(xk_pad[:].bitcast(F32), 0.0)
            for p in range(2):
                nc.gpsimd.memset(xv[p][:], 0.0).then_inc(const_ready, 1)
            pool.wait_ge(const_ready, 2)
            for p in range(2):
                nc.gpsimd.memset(xv[p][:, :, XK:XK + 1], 1.0).then_inc(const_ready, 1)
            pool.wait_ge(w_loaded, 16 * len(small))

            def norm_fill(b, n):
                pool.wait_ge(summed, 4 * b + n + 1)
                nc.gpsimd.tensor_tensor(prob[:, n], prob[:, n], recip[:, n, :, None].broadcast_to([128, 4, S]),
                                        ALU.mult).then_inc(normed, 1)

            def rope_sin(s, n):
                drained(pool, s, f"f.Q{n}")
                part = qk[:, 8 * n:8 * n + 8, 0:ROPE].rearrange("p h (a i) -> p h a i", a=2)
                sines = qk_sin[:, 8 * n:8 * n + 8, :].rearrange("p h (a i) -> p h a i", a=2)
                for side in range(2):
                    table = sin_sb[:, None, side * ROPE // 2:(side + 1) * ROPE // 2].broadcast_to([128, 8, ROPE // 2])
                    last = nc.gpsimd.tensor_tensor(sines[:, :, side, :], part[:, :, 1 - side, :], table, ALU.mult)
                last.then_inc(sin_done, 1)

            def rope_add(b, n):
                pool.wait_ge(sin_done, 4 * b + n + 1)
                pool.wait_ge(cos_done, 4 * b + n + 1)
                nc.gpsimd.tensor_tensor(qk[:, 8 * n:8 * n + 8, 0:ROPE], qk_cos[:, 8 * n:8 * n + 8, :],
                                        qk_sin[:, 8 * n:8 * n + 8, :], ALU.add).then_inc(roped, 1)

            def cross_add(b):
                pool.wait_ge(xt_ready, b + 1)
                nc.gpsimd.tensor_tensor(xr[:], xt1[:], xt2[:], ALU.add).then_inc(xr_ready, 1)

            def rstd(b, mv, ve, out_, mv_ready, ve_ready, done):
                pool.wait_ge(mv_ready, b + 1)
                nc.gpsimd.tensor_tensor(ve[:], mv[:, 1:2], eps[:, 0:1], ALU.add).then_inc(ve_ready, 1)
                pool.wait_ge(ve_ready, b + 1)
                nc.gpsimd.tensor_tensor(out_[:], ve[:], mhalf[:, 0:1], ALU.pow).then_inc(done, 1)

            def slot(s, p, f, k, a, c):
                if on(a):
                    rstd(a, mv1, ve1, rstd1, mv1_ready, ve1_ready, rstd1_ready)
                if on(k):
                    norm_fill(k, 0)
                    norm_fill(k, 1)
                    norm_fill(k, 2)
                if on(a):
                    cross_add(a)
                if on(k):
                    norm_fill(k, 3)
                if on(f):
                    rope_sin(s, 0)
                    rope_sin(s, 1)
                    rope_add(f, 0)
                    rope_add(f, 1)
                    rope_sin(s, 2)
                if on(c):
                    rstd(c, mv2, ve2, rstd2, mv2_ready, ve2_ready, rstd2_ready)
                if on(f):
                    rope_add(f, 2)
                    rope_sin(s, 3)
                    rope_add(f, 3)

            slots(pool, slot)

        @block.scalar
        def _(act):
            def copy(s, name, dst, scale=1.0, n=COLS):
                filled(act, s, name)
                nc.scalar.activation(dst, bank(name, n), ACT.Copy, scale=scale).then_inc(ring.drained[ring.bank(name)], 1)

            for half in range(2):
                act.wait_ge(wqkv_loaded, 16 * 3)
                nc.scalar.activation(w_hi[:, half * QKV // 2:(half + 1) * QKV // 2], stage[half],
                                     ACT.Copy).then_inc(w_hi_ready, 1)

            def exp_fill(s, b, n):
                name = f"k.S{n}"
                act.wait_ge(maxed, 4 * b + n + 1)
                for j in range(4):
                    last = nc.scalar.activation(prob[:, n, j, :], bank(name)[:, j * S:(j + 1) * S], ACT.Exp,
                                                bias=negmax[:, n, j:j + 1], accum_out=sums[:, n, j:j + 1])
                last.then_inc(ring.drained[ring.bank(name)], 1)

            def xexp_fill(s, b, n):
                name = f"a.S{n}"
                act.wait_ge(xmaxed, 4 * b + n + 1)
                for g in range(XG):
                    last = nc.scalar.activation(xprob[:, n, g, :], bank(name)[:, g * S:(g + 1) * S], ACT.Exp,
                                                bias=xmax[:, n, g:g + 1])
                last.then_inc(ring.drained[ring.bank(name)], 1)

            def q_copy(s, n):
                copy(s, f"f.Q{n}", qk[:, 8 * n:8 * n + 8, :].rearrange("p h k -> p (h k)"), DK ** -0.5 if n < 2 else 1.0)

            def cross_hi(b):
                act.wait_ge(xr_ready, b + 1)
                nc.scalar.activation(xq_parts[:, :, 0:2, 0:XK], xr[:, 0:XH, None, :].broadcast_to([128, XH, 2, XK]),
                                     ACT.Copy, scale=qm[:, 0:1])
                nc.scalar.activation(xk_parts[:, :, 0:3:2, 0:XK], xr[:, XH:XH + XG, None, :].broadcast_to([128, XG, 2, XK]),
                                     ACT.Copy).then_inc(xhi_ready, 1)

            def slot(s, p, f, k, a, c):
                if on(c):
                    copy(s, "c.PT0", xprobT[:, 0].rearrange("p j s -> p (j s)"))
                if on(f):
                    if isinstance(s, int) and s == 0:
                        act.wait_ge(w_lo_ready, 2)
                    filled(act, s, "f.XT")
                    nc.scalar.activation(xT_hi[:], bank("f.XT", S), ACT.Copy).then_inc(x_hi_ready, 1)
                if on(a):
                    copy(s, "a.T", xcT[:].rearrange("p a s -> p (a s)"), n=2 * S)
                if on(k):
                    exp_fill(s, k, 0)
                    exp_fill(s, k, 1)
                    exp_fill(s, k, 2)
                    exp_fill(s, k, 3)
                if on(f):
                    q_copy(s, 0)
                if on(a):
                    cross_hi(a)
                if on(f):
                    q_copy(s, 1)
                    q_copy(s, 3)
                    q_copy(s, 2)
                if on(a):
                    copy(s, "a.QT", xqT[:].rearrange("p c s -> p (c s)"))
                if on(k):
                    copy(s, "k.PT2", probT[:, 2].rearrange("p j s -> p (j s)"))
                if on(f):
                    copy(s, "f.Q4", v[p][:, 0:COLS])
                if on(k):
                    copy(s, "k.PT3", probT[:, 3].rearrange("p j s -> p (j s)"))
                    copy(s, "k.OT0", oT[:, 0:4, :].rearrange("p c s -> p (c s)"))
                if on(f):
                    copy(s, "f.T1", qT[p][:, 4:8, :].rearrange("p c s -> p (c s)"))
                if on(a):
                    xexp_fill(s, a, 0)
                if on(k):
                    copy(s, "k.OT1", oT[:, 4:8, :].rearrange("p c s -> p (c s)"))
                if on(a):
                    xexp_fill(s, a, 1)
                if on(f):
                    copy(s, "f.T2", kT[p][:, 0:4, :].rearrange("p c s -> p (c s)"))
                if on(a):
                    xexp_fill(s, a, 2)
                if on(f):
                    copy(s, "f.T3", kT[p][:, 4:8, :].rearrange("p c s -> p (c s)"))
                if on(a):
                    xexp_fill(s, a, 3)

            slots(act, slot)

        @block.vector
        def _(dve):
            def copy(s, name, dst, n=COLS):
                filled(dve, s, name)
                nc.vector.tensor_copy(dst, bank(name, n)).then_inc(ring.drained[ring.bank(name)], 1)

            for half in range(2):
                dve.wait_ge(w_hi_ready, half + 1)
                part = slice(half * QKV // 2, (half + 1) * QKV // 2)
                nc.vector.tensor_tensor(w_lo[:, part], stage[half], w_hi[:, part].bitcast(F32),
                                        ALU.subtract).then_inc(w_lo_ready, 1)
            dve.wait_ge(w_loaded, 16 * len(small))
            nc.vector.tensor_copy(qm_all[:], qm_u8[:])
            nc.vector.tensor_copy(identb[:], ident[:])
            nc.vector.tensor_copy(causal[:], causal_f[:, None, :].broadcast_to([128, 4, 128]))
            nc.vector.tensor_scalar(kb_all[:], kp_u8[:], -1.0, BIG, ALU.add, ALU.mult).then_inc(masks_made, 1)
            dve.wait_ge(masks_made, 1)
            dve.wait_ge(const_ready, 4)

            def scores_max(s, name, dst, done):
                filled(dve, s, name)
                nc.vector.tensor_reduce(dst, bank(name).rearrange("p (j s) -> p j s", j=4), AX_X, ALU.max,
                                        negate=True).then_inc(done, 1)

            def recip_fill(s, n):
                drained(dve, s, f"k.S{n}")
                nc.vector.reciprocal(recip[:, n, :], sums[:, n, :]).then_inc(summed, 1)

            def rope_cos(s, n):
                drained(dve, s, f"f.Q{n}")
                nc.vector.tensor_tensor(qk_cos[:, 8 * n:8 * n + 8, :], qk[:, 8 * n:8 * n + 8, 0:ROPE],
                                        cos_sb[:, None, :].broadcast_to([128, 8, ROPE]), ALU.mult).then_inc(cos_done, 1)

            def residual(s, name, y, old, st, done):
                filled(dve, s, name)
                nc.vector.tensor_tensor(y[:], bank(name, D), old[:], ALU.add).then_inc(ring.drained[ring.bank(name)], 1)
                drained(dve, s, name)
                nc.vector.bn_stats(st[:], y[:]).then_inc(done, 1)

            def moments(b, st, mv, st_ready, done):
                dve.wait_ge(st_ready, b + 1)
                nc.vector.memset(scratch[:], 0.0)
                nc.vector.bn_aggr(mv[:], st[:]).then_inc(done, 1)

            def normalise(b, y, mv, rs, dst, kept, rs_ready, done):
                dve.wait_ge(rs_ready, b + 1)
                for d in (dst, kept):
                    last = nc.vector.tensor_scalar(d, y[:], mv[:, 0:1], rs[:, 0:1], ALU.subtract, ALU.mult)
                last.then_inc(done, 1)

            def x_lo(s, b):
                dve.wait_ge(x_hi_ready, b + 1)
                nc.vector.tensor_tensor(xT_lo[:], bank("f.XT", S), xT_hi[:].bitcast(F32),
                                        ALU.subtract).then_inc(ring.drained[ring.bank("f.XT")], 1)

            def cross_k(s):
                filled(dve, s, "a.KT")
                nc.vector.tensor_tensor(xkT[:], bank("a.KT", S)[:, None, :].broadcast_to([128, XG, S]),
                                        gsel[:, :, None].broadcast_to([128, XG, S]), ALU.mult)\
                    .then_inc(ring.drained[ring.bank("a.KT")], 1)

            def divide(s, b):
                filled(dve, s, "c.O")
                o = bank("c.O").rearrange("p (c g r) -> p c g r", c=GRP, g=XG)
                nc.vector.reciprocal(xrec[:], o[:, :, :, XK]).then_inc(xrec_ready, 1)
                dve.wait_ge(xrec_ready, b + 1)
                nc.vector.tensor_tensor(xo[:].rearrange("p (c g k) -> p c g k", g=XG, c=GRP), o[:, :, :, 0:XK],
                                        xrec[:, :, :, None].broadcast_to([128, GRP, XG, XK]), ALU.mult)\
                    .then_inc(ring.drained[ring.bank("c.O")], 1)

            def split_x2(s, b):
                drained(dve, s, "c.XT")
                hi = x2T_hi[:, bass.ds(b * S, S)]
                nc.vector.tensor_copy(hi, x2T[:]).then_inc(x2_hi_ready, 1)
                dve.wait_ge(x2_hi_ready, b + 1)
                nc.vector.tensor_tensor(x2T_lo[:, bass.ds(b * S, S)], x2T[:], hi.bitcast(F32), ALU.subtract).then_inc(x2_split, 1)

            def add_bias(s, b):
                filled(dve, s, "c.R")
                nc.vector.tensor_tensor(logits[:, bass.ds(b, 1), :].rearrange("p a e -> p (a e)"),
                                        bank("c.R", E), rb_sb[:], ALU.add).then_inc(ring.drained[ring.bank("c.R")], 1)

            def cross_rope(s, b, p):
                filled(dve, s, "a.QKV")
                flat = bank("a.QKV", (XH + XG) * XK)
                src = flat.rearrange("p (h a i) -> p h a i", a=2, i=XK // 2)
                nc.vector.tensor_copy(qm[:], qm_all[:, bass.ds(b, 1)])
                nc.vector.tensor_tensor(xt1[:].rearrange("p h k -> p (h k)"), flat, xcos_sb[:].rearrange("p h k -> p (h k)"),
                                        ALU.mult)
                t2 = xt2[:].rearrange("p h (a i) -> p h a i", a=2)
                sn = xsin_sb[:].rearrange("p h (a i) -> p h a i", a=2)
                for side in range(2):
                    last = nc.vector.tensor_tensor(t2[:, :, side, :], src[:, :, 1 - side, :], sn[:, :, side, :], ALU.mult)
                last.then_inc(xt_ready, 1)
                nc.vector.tensor_copy(xv[p][:, :, 0:XK], bank("a.QKV")[:, 160:192].rearrange("p (g k) -> p g k", g=XG))\
                    .then_inc(ring.drained[ring.bank("a.QKV")], 1)

            def cross_lo(b):
                dve.wait_ge(xhi_ready, b + 1)
                nc.vector.scalar_tensor_tensor(xq_parts[:, :, 2, 0:XK], xr[:, 0:XH], qm[:, 0:1],
                                               xq_parts[:, :, 0, 0:XK].bitcast(F32), ALU.mult, ALU.subtract)
                nc.vector.tensor_tensor(xk_parts[:, :, 1, 0:XK], xr[:, XH:XH + XG], xk_parts[:, :, 0, 0:XK].bitcast(F32),
                                        ALU.subtract)
                nc.vector.tensor_copy(xk_parts[:, :, 0, XK], kb_all[:, bass.ds(b, 1)].broadcast_to([128, XG]))
                nc.vector.tensor_copy(xq_parts[:, :, 0, XK], qm[:, 0:1].broadcast_to([128, XH])).then_inc(xlo_ready, 1)

            def slot(s, p, f, k, a, c):
                if on(a):
                    dve.wait_ge(xres_loaded[p], loads(a, p))
                    residual(s - 1, "k.Y", y1, xres[p], st1, st1_ready)
                    moments(a, st1, mv1, st1_ready, mv1_ready)
                if on(c):
                    copy(s, "c.PT1", xprobT[:, 1].rearrange("p j s -> p (j s)"))
                if on(a):
                    normalise(a, y1, mv1, rstd1, x1[:], x1c[p][:], rstd1_ready, x1_ready)
                if on(k):
                    scores_max(s, "k.S0", negmax[:, 0, :], maxed)
                    scores_max(s, "k.S1", negmax[:, 1, :], maxed)
                if on(c):
                    copy(s, "c.PT2", xprobT[:, 2].rearrange("p j s -> p (j s)"))
                    copy(s, "c.PT3", xprobT[:, 3].rearrange("p j s -> p (j s)"))
                if on(k):
                    recip_fill(s, 0)
                    scores_max(s, "k.S2", negmax[:, 2, :], maxed)
                if on(f):
                    x_lo(s, f)
                if on(k):
                    recip_fill(s, 1)
                    scores_max(s, "k.S3", negmax[:, 3, :], maxed)
                if on(c):
                    copy(s, "c.OT", xoT[:].rearrange("p c s -> p (c s)"))
                if on(k):
                    recip_fill(s, 2)
                if on(a):
                    cross_rope(s, a, p)
                if on(k):
                    copy(s, "k.PT0", probT[:, 0].rearrange("p j s -> p (j s)"))
                    recip_fill(s, 3)
                if on(c):
                    divide(s, c)
                if on(f):
                    rope_cos(s, 0)
                if on(c):
                    copy(s, "c.T", xonT[:], n=S)
                if on(a):
                    cross_lo(a)
                if on(k):
                    copy(s, "k.PT1", probT[:, 1].rearrange("p j s -> p (j s)"))
                if on(a):
                    cross_k(s)
                if on(f):
                    rope_cos(s, 1)
                if on(c):
                    residual(s, "c.Y", y2, x1c[1 - p], st2, st2_ready)
                    moments(c, st2, mv2, st2_ready, mv2_ready)
                if on(a):
                    scores_max(s, "a.S0", xmax[:, 0, :], xmaxed)
                if on(f):
                    copy(s, "f.T0", qT[p][:, 0:4, :].rearrange("p c s -> p (c s)"))
                    rope_cos(s, 2)
                if on(a):
                    scores_max(s, "a.S1", xmax[:, 1, :], xmaxed)
                if on(c):
                    normalise(c, y2, mv2, rstd2, x2[:], x2_all[:, bass.ds(c, 1), :].rearrange("p a d -> p (a d)"), rstd2_ready, x2_ready)
                if on(a):
                    scores_max(s, "a.S2", xmax[:, 2, :], xmaxed)
                if on(f):
                    rope_cos(s, 3)
                if on(c):
                    copy(s, "c.XT", x2T[:], n=S)
                if on(f):
                    copy(s, "f.Q5", v[p][:, COLS:2 * COLS])
                if on(c):
                    split_x2(s, c)
                    add_bias(s, c)
                if on(a):
                    scores_max(s, "a.S3", xmax[:, 3, :], xmaxed)

            slots(dve, slot)

        @block.tensor
        def _(pe):
            def transpose(dst, src):
                return nc.tensor.transpose(dst, src, ident[:])

            pe.wait_ge(wqkv_loaded, 16)
            pe.wait_ge(w_loaded, 16 * len(small))
            pe.wait_ge(masks_made, 1)
            pe.wait_ge(const_ready, 4)

            def slot(s, p, f, k, a, c):
                q = 1 - p

                def free(name):
                    wait(pe, ring.drained[ring.bank(name)], ring.count(s, name) - 1)
                    return bank(name)

                def done(name, last):
                    last.then_inc(ring.filled[ring.bank(name)], 1)

                def x_transpose():
                    pe.wait_ge(xf_loaded[p], loads(f, p))
                    done("f.XT", transpose(free("f.XT")[:, 0:S], xf[p][:]))

                def qkv(n):
                    if n == 0:
                        drained(pe, s, "f.XT")
                    dst = free(f"f.Q{n}")
                    cols = slice(n * COLS, (n + 1) * COLS)
                    nc.tensor.matmul(dst, xT_hi[:], w_lo[:, cols], start=True, stop=False)
                    nc.tensor.matmul(dst, xT_lo[:], w_hi[:, cols], start=False, stop=False)
                    done(f"f.Q{n}", nc.tensor.matmul(dst, xT_hi[:], w_hi[:, cols], start=False, stop=True))

                def qk_transpose(n):
                    pe.wait_ge(roped, 4 * f + n + 1)
                    dst = free(f"f.T{n}")
                    for j in range(4):
                        last = transpose(dst[:, j * S:(j + 1) * S],
                                         qk[:, 8 * n + 2 * j:8 * n + 2 * j + 2, :].rearrange("p h k -> p (h k)"))
                    done(f"f.T{n}", last)

                def scores(u):
                    names = [f"k.S{2 * u + r}" for r in range(2)]
                    if u == 0:
                        for n in range(4):
                            drained(pe, s - 1, f"f.T{n}")
                    dst = [free(name) for name in names]
                    for r in range(2):
                        nc.tensor.matmul(dst[r], identb[:], causal[:].rearrange("p j s -> p (j s)"), start=True, stop=False,
                                         skip_group_check=True)
                    for j in range(4):
                        for r in range(2):
                            rows = slice(64 * r, 64 * r + 64)
                            last = nc.tensor.matmul(dst[r][:, j * S:(j + 1) * S], qT[q][rows, 4 * u + j, :],
                                                    kT[q][rows, 4 * u + j, :], start=False, stop=(j == 3),
                                                    skip_group_check=True)
                            if j == 3:
                                done(names[r], last)

                def prob_transpose(n):
                    pe.wait_ge(normed, 4 * k + n + 1)
                    dst = free(f"k.PT{n}")
                    for j in range(4):
                        last = transpose(dst[:, j * S:(j + 1) * S], prob[:, n, j, :])
                    done(f"k.PT{n}", last)

                def pv(u):
                    for r in range(2):
                        drained(pe, s, f"k.PT{2 * u + r}")
                    dst = free(f"k.OT{u}")
                    for j in range(4):
                        for r in range(2):
                            h = 2 * (4 * u + j) + r
                            last = nc.tensor.matmul(dst[64 * r:64 * r + 64, j * S:(j + 1) * S],
                                                    v[q][:, h * DK:(h + 1) * DK], probT[:, 2 * u + r, j, :],
                                                    start=True, stop=True)
                    done(f"k.OT{u}", last)

                def out_proj():
                    for u in range(2):
                        drained(pe, s, f"k.OT{u}")
                    dst = free("k.Y")
                    for n in range(CH):
                        last = nc.tensor.matmul(dst[:, 0:D], oT[:, n, :], wo_sb[:, n, :], start=(n == 0), stop=(n == CH - 1))
                    done("k.Y", last)

                def xc_transpose():
                    pe.wait_ge(x1_ready, a + 1)
                    pe.wait_ge(cx_loaded[p], loads(a, p))
                    dst = free("a.T")
                    transpose(dst[:, 0:S], x1[:])
                    done("a.T", transpose(dst[:, S:2 * S], cx[p][:]))

                def xqkv():
                    drained(pe, s, "a.T")
                    dst = free("a.QKV")
                    nc.tensor.matmul(dst[:, 0:128], xcT[:, 0, :], xwq_sb[:], start=True, stop=True)
                    done("a.QKV", nc.tensor.matmul(dst[:, 128:192], xcT[:, 1, :], xwkv_sb[:], start=True, stop=True))

                def xqk_transpose():
                    pe.wait_ge(xlo_ready, a + 1)
                    dst = free("a.QT")
                    for j in range(GRP):
                        last = transpose(dst[:, j * S:(j + 1) * S], xq_pad[:, j].bitcast(F32))
                    done("a.QT", last)
                    done("a.KT", transpose(free("a.KT")[:, 0:S], xk_pad[:].bitcast(F32)))

                def xscores(n):
                    if n == 0:
                        drained(pe, s, "a.QT")
                        drained(pe, s, "a.KT")
                    done(f"a.S{n}", nc.tensor.matmul(free(f"a.S{n}"), xqT[:, n, :], xkT[:].rearrange("p g s -> p (g s)"),
                                                     start=True, stop=True))

                def xprob_transpose(n):
                    drained(pe, s - 1, f"a.S{n}")
                    dst = free(f"c.PT{n}")
                    for g in range(XG):
                        last = transpose(dst[:, g * S:(g + 1) * S], xprob[:, n, g, :])
                    done(f"c.PT{n}", last)

                def xpv():
                    for n in range(4):
                        drained(pe, s, f"c.PT{n}")
                    dst = free("c.OT")
                    for g in range(XG):
                        last = nc.tensor.matmul(dst[32 * g:32 * g + 32, :], xv[q][:, g, :], xprobT[:, :, g, :],
                                                start=True, stop=True, skip_group_check=True)
                    done("c.OT", last)

                def xo_back():
                    drained(pe, s, "c.OT")
                    dst = free("c.O")
                    for j in range(GRP):
                        last = transpose(dst[:, j * S:(j + 1) * S], xoT[:, j, :])
                    done("c.O", last)

                def xo_transpose():
                    drained(pe, s, "c.O")
                    done("c.T", transpose(free("c.T")[:, 0:S], xo[:]))

                def xout():
                    drained(pe, s, "c.T")
                    done("c.Y", nc.tensor.matmul(free("c.Y")[:, 0:D], xonT[:], xwo_sb[:], start=True, stop=True))

                def x2_transpose():
                    pe.wait_ge(x2_ready, c + 1)
                    done("c.XT", transpose(free("c.XT")[:, 0:S], x2[:]))

                def router():
                    drained(pe, s, "c.XT")
                    done("c.R", nc.tensor.matmul(free("c.R")[:, 0:E], x2T[:], rw_sb[:], start=True, stop=True))

                if on(c):
                    xprob_transpose(0)
                    xprob_transpose(1)
                if on(k):
                    scores(0)
                if on(f):
                    x_transpose()
                if on(a):
                    xc_transpose()
                if on(c):
                    xprob_transpose(2)
                    xprob_transpose(3)
                if on(k):
                    scores(1)
                if on(c):
                    xpv()
                if on(a):
                    xqkv()
                if on(k):
                    prob_transpose(0)
                if on(f):
                    if isinstance(s, int) and s == 0:
                        pe.wait_ge(w_lo_ready, 2)
                    qkv(0)
                    qkv(1)
                if on(c):
                    xo_back()
                if on(f):
                    qkv(2)
                    qkv(3)
                if on(k):
                    prob_transpose(1)
                if on(c):
                    xo_transpose()
                if on(f):
                    qkv(4)
                if on(k):
                    prob_transpose(2)
                if on(a):
                    xqk_transpose()
                if on(c):
                    xout()
                if on(k):
                    prob_transpose(3)
                    pv(0)
                if on(a):
                    xscores(0)
                if on(f):
                    qk_transpose(0)
                    qk_transpose(1)
                if on(a):
                    xscores(1)
                if on(k):
                    pv(1)
                if on(f):
                    qkv(5)
                if on(a):
                    xscores(2)
                if on(f):
                    qk_transpose(2)
                if on(c):
                    x2_transpose()
                if on(k):
                    out_proj()
                if on(a):
                    xscores(3)
                if on(c):
                    router()
                if on(f):
                    qk_transpose(3)

            slots(pe, slot)


def ffn_phase(nc, sem, ps, x2_all, x2T_hi, x2T_lo, logits, ident, mhalf, eps, scratch, temp, eidx, fwg, fwp, fwo, out):
    NF = E * FF // 128
    with ExitStack() as phase:
        def sb(name, shape, dt=F32):
            return phase.enter_context(nc.sbuf_tensor(name, shape, dt))

        stage = [sb(f"fstage{i}", [128, E * FF]) for i in range(2)]
        w_hi = [sb(f"fw_hi{i}", [128, E * FF], F32R) for i in range(2)]
        w_lo = [sb(f"fw_lo{i}", [128, E * FF], F32R) for i in range(2)]
        wo_sb = sb("fwo_sb", [128, NF, D])
        temp_sb = sb("temp_sb", [128, 1])
        eidx_sb = sb("eidx_sb", [128, E])
        rtemp = sb("rtemp", [128, 2])
        la = sb("la", [128, B, E])
        laT = sb("laT", [128, 2, S])
        dif = sb("dif", [128, B, E])
        ex = sb("ex", [128, B, E])
        exT = sb("exT", [128, 2, S])
        rmax = sb("rmax", [128, B])
        rsum = sb("rsum", [128, B])
        rlog = sb("rlog", [128, B])
        cmax = sb("cmax", [128, 2])
        csum = sb("csum", [128, 2])
        clog = sb("clog", [128, 2])
        gates = sb("gates", [128, B, E])
        cand = sb("cand", [128, B, E])
        one = [sb(f"one{i}", [128, B, E]) for i in range(2)]
        top = [sb(f"top{i}", [128, B]) for i in range(2)]
        low = sb("low", [128, B])
        wts = sb("wts", [128, B, E])
        gs = [sb(f"gs{i}", [128, FB * S]) for i in range(2)]
        h = [sb(f"h{i}", [128, FB * S]) for i in range(4)]
        part = [sb(f"part{i}", [128, FB, D]) for i in range(2)]
        acc = sb("acc", [128, FB, D])
        st3 = sb("st3", [128, FB, 6])
        mv3 = sb("mv3", [128, FB, 2])
        ve3 = sb("ve3", [128, FB])
        rstd3 = sb("rstd3", [128, FB])
        yo = sb("yo", [128, FB, D])

        up = Ring(sem, "up", [0, 1, 2, 3], 2 * NF)
        down = Ring(sem, "down", [4, 5], E)
        f_loaded = sem("f_loaded")
        fc_loaded = sem("fc_loaded")
        fo_loaded = sem("fo_loaded")
        f_hi = sem("f_hi")
        f_lo = sem("f_lo")
        sk_dve = sem("sk_dve")
        sk_act = sem("sk_act")
        sk_scaled = sem("sk_scaled")
        sk_pe = sem("sk_pe")
        acc_done = sem("acc_done")
        st3_ready = sem("st3_ready")
        mv3_ready = sem("mv3_ready")
        ve3_ready = sem("ve3_ready")
        rstd3_ready = sem("rstd3_ready")
        yo_ready = sem("yo_ready")
        stored = sem("stored")

        there, again = ps[:, 6, 0:2 * S], ps[:, 7, 0:2 * S]
        flat = lambda t: t[:].rearrange("p b e -> p (b e)")
        over_e = lambda t: t[:, :, None].broadcast_to([128, B, E])

        def groups(eng, group):
            group(0)
            with eng.Fori(1, B // FB) as g:
                group(g)

        DS, AS, PS = 6, 4, 2

        block = phase.enter_context(nc.Block())

        @block.sync
        def _(sp):
            sp.dma_start(temp_sb[:], temp).then_inc(fc_loaded, 16)
            sp.dma_start(eidx_sb[:], eidx).then_inc(fc_loaded, 16)
            sp.dma_start(stage[0][:], fwg).then_inc(f_loaded, 16)
            sp.dma_start(stage[1][:], fwp).then_inc(f_loaded, 16)
            sp.dma_start(wo_sb[:], fwo.rearrange("(n p) d -> p n d", p=128)).then_inc(fo_loaded, 16)

            def group(g):
                sp.wait_ge(yo_ready, FB * (g + 1))
                sp.dma_start(out[bass.ds(g * FB, FB), :, :].rearrange("a s d -> s a d"), yo[:]).then_inc(stored, 16)

            groups(sp, group)
            sp.wait_ge(stored, 16 * (B // FB))

        @block.gpsimd
        def _(pool):
            for i in range(2):
                pool.wait_ge(f_hi, i + 1)
                nc.gpsimd.tensor_tensor(w_lo[i][:], stage[i][:], w_hi[i][:].bitcast(F32), ALU.subtract).then_inc(f_lo, 1)

            def group(g):
                for e in range(E):
                    pool.wait_ge(down.drained[e % 2], down.count(g, e))
                    if e == 0:
                        wait(pool, yo_ready, FB * g)
                        own = x2_all[:, bass.ds(g * FB, FB), :]
                        nc.gpsimd.tensor_tensor(acc[:], own, own, ALU.add).then_inc(acc_done, 1)
                    pool.wait_ge(acc_done, (E + 1) * g + e + 1)
                    nc.gpsimd.tensor_tensor(acc[:], acc[:], part[e % 2][:], ALU.add).then_inc(acc_done, 1)
                pool.wait_ge(mv3_ready, FB * (g + 1))
                nc.gpsimd.tensor_tensor(ve3[:], mv3[:, :, 1], eps[:], ALU.add).then_inc(ve3_ready, 1)
                pool.wait_ge(ve3_ready, g + 1)
                nc.gpsimd.tensor_tensor(rstd3[:], ve3[:], mhalf[:], ALU.pow).then_inc(rstd3_ready, 1)

            groups(pool, group)

        @block.scalar
        def _(act):
            for i in range(2):
                act.wait_ge(f_loaded, 32)
                nc.scalar.activation(w_hi[i][:], stage[i][:], ACT.Copy).then_inc(f_hi, 1)
            for it in range(SINKHORN_ITERS):
                act.wait_ge(sk_dve, 2 + DS * it + 2)
                nc.scalar.activation(flat(ex), flat(dif), ACT.Exp).then_inc(sk_act, 1)
                act.wait_ge(sk_dve, 2 + DS * it + 3)
                nc.scalar.activation(rlog[:], rsum[:], ACT.Ln).then_inc(sk_act, 1)
                act.wait_ge(sk_dve, 2 + DS * it + 5)
                for j in range(2):
                    last = nc.scalar.activation(exT[:, j, :], there[:, j * S:(j + 1) * S], ACT.Exp, bias=cmax[:, j:j + 1],
                                                accum_out=csum[:, j:j + 1])
                last.then_inc(sk_act, 1)
                act.wait_ge(sk_act, AS * it + 3)
                nc.scalar.activation(clog[:], csum[:], ACT.Ln).then_inc(sk_act, 1)
            act.wait_ge(sk_pe, PS * SINKHORN_ITERS)
            nc.scalar.activation(flat(ex), again, ACT.Exp).then_inc(sk_act, 1)

            def group(g):
                for n in range(NF):
                    act.wait_ge(up.filled[(2 * n) % 4], up.count(g, 2 * n))
                    wait(act, up.drained[(2 * n + 1) % 4], up.count(g, 2 * n + 1) - 1)
                    nc.scalar.activation(gs[n % 2][:], ps[:, up.bank(2 * n), :], ACT.Relu)\
                        .then_inc(up.drained[(2 * n) % 4], 1)

            groups(act, group)

        @block.vector
        def _(dve):
            steps = [0]

            def link(ins):
                steps[0] += 1
                ins.then_inc(sk_dve, 1)
                dve.wait_ge(sk_dve, steps[0])

            dve.wait_ge(fc_loaded, 32)
            link(nc.vector.tensor_scalar(rtemp[:, 0:1], temp_sb[:], 0.1, None, ALU.max))
            link(nc.vector.reciprocal(rtemp[:, 1:2], rtemp[:, 0:1]))
            sc_step = nc.vector.tensor_scalar(flat(la), flat(logits), rtemp[:, 1:2], None, ALU.mult)
            for it in range(SINKHORN_ITERS):
                if it == 0:
                    sc_step.then_inc(sk_scaled, 1)
                    dve.wait_ge(sk_scaled, 1)
                    src = la[:]
                else:
                    dve.wait_ge(sk_pe, PS * it)
                    src = again.rearrange("p (b e) -> p b e", b=B)
                link(nc.vector.tensor_reduce(rmax[:], src, AX_X, ALU.max))
                link(nc.vector.tensor_tensor(dif[:], src, over_e(rmax), ALU.subtract))
                dve.wait_ge(sk_act, AS * it + 1)
                link(nc.vector.tensor_reduce(rsum[:], ex[:], AX_X, ALU.add))
                dve.wait_ge(sk_act, AS * it + 2)
                link(nc.vector.tensor_tensor(la[:], dif[:], over_e(rlog), ALU.subtract))
                dve.wait_ge(sk_pe, PS * it + 1)
                link(nc.vector.tensor_reduce(cmax[:], there.rearrange("p (j s) -> p j s", j=2), AX_X, ALU.max, negate=True))
                dve.wait_ge(sk_act, AS * it + 4)
                for j in range(2):
                    last = nc.vector.tensor_scalar(laT[:, j, :], there[:, j * S:(j + 1) * S], cmax[:, j:j + 1],
                                                   clog[:, j:j + 1], ALU.add, ALU.subtract)
                link(last)
            dve.wait_ge(sk_act, AS * SINKHORN_ITERS + 1)
            link(nc.vector.tensor_reduce(rsum[:], ex[:], AX_X, ALU.add))
            link(nc.vector.tensor_scalar(rlog[:], rsum[:], 1e-8, None, ALU.add))
            link(nc.vector.reciprocal(rmax[:], rlog[:]))
            link(nc.vector.tensor_tensor(gates[:], ex[:], over_e(rmax), ALU.mult))
            src = gates
            idx = eidx_sb[:, None, :].broadcast_to([128, B, E])
            for i in range(2):
                link(nc.vector.tensor_reduce(top[i][:], src[:], AX_X, ALU.max))
                link(nc.vector.tensor_tensor(cand[:], src[:], over_e(top[i]), ALU.is_equal))
                link(nc.vector.tensor_tensor(cand[:], cand[:], idx, ALU.mult))
                link(nc.vector.tensor_reduce(low[:], cand[:], AX_X, ALU.min))
                link(nc.vector.tensor_tensor(one[i][:], cand[:], over_e(low), ALU.is_equal))
                if i == 0:
                    link(nc.vector.scalar_tensor_tensor(flat(dif), flat(one[0]), -4.0, flat(gates), ALU.mult, ALU.add))
                    src = dif
            link(nc.vector.scalar_tensor_tensor(rsum[:], top[0][:], 1e-8, top[1][:], ALU.add, ALU.add))
            link(nc.vector.reciprocal(rlog[:], rsum[:]))
            link(nc.vector.tensor_tensor(cand[:], one[0][:], one[1][:], ALU.add))
            link(nc.vector.tensor_tensor(ex[:], cand[:], gates[:], ALU.mult))
            link(nc.vector.tensor_tensor(wts[:], ex[:], over_e(rlog), ALU.mult))

            def hidden(g, n):
                dve.wait_ge(up.filled[(2 * n + 1) % 4], up.count(g, 2 * n + 1))
                dve.wait_ge(up.drained[(2 * n) % 4], up.count(g, 2 * n))
                if n % 2 == 0:
                    wait(dve, down.filled[(n // 2) % 2], down.count(g, n // 2) - 1)
                nc.vector.tensor_tensor(h[n % 4][:], ps[:, up.bank(2 * n + 1), :], gs[n % 2][:], ALU.mult)\
                    .then_inc(up.drained[(2 * n + 1) % 4], 1)

            def combine(g, e):
                dve.wait_ge(down.filled[e % 2], down.count(g, e))
                if not isinstance(g, int) or e >= 2:
                    wait(dve, acc_done, (E + 1) * g + e)
                nc.vector.tensor_tensor(part[e % 2][:], ps[:, down.bank(e), :].rearrange("p (b d) -> p b d", b=FB),
                                        wts[:, bass.ds(g * FB, FB), e:e + 1].broadcast_to([128, FB, D]), ALU.mult)\
                    .then_inc(down.drained[e % 2], 1)

            def group(g):
                for e in range(E):
                    hidden(g, 2 * e)
                    hidden(g, 2 * e + 1)
                    if e:
                        combine(g, e - 1)
                combine(g, E - 1)
                dve.wait_ge(acc_done, (E + 1) * (g + 1))
                for b in range(FB):
                    nc.vector.bn_stats(st3[:, b, :], acc[:, b, :]).then_inc(st3_ready, 1)
                dve.wait_ge(st3_ready, FB * (g + 1))
                nc.vector.memset(scratch[:], 0.0)
                for b in range(FB):
                    nc.vector.bn_aggr(mv3[:, b, :], st3[:, b, :]).then_inc(mv3_ready, 1)
                dve.wait_ge(rstd3_ready, g + 1)
                wait(dve, stored, 16 * g)
                for b in range(FB):
                    nc.vector.tensor_scalar(yo[:, b, :], acc[:, b, :], mv3[:, b, 0:1], rstd3[:, b:b + 1],
                                            ALU.subtract, ALU.mult).then_inc(yo_ready, 1)

            groups(dve, group)

        @block.tensor
        def _(pe):
            for it in range(SINKHORN_ITERS):
                pe.wait_ge(sk_dve, 2 + DS * it + 4)
                for j in range(2):
                    last = nc.tensor.transpose(there[:, j * S:(j + 1) * S], flat(la)[:, j * 128:(j + 1) * 128], ident[:])
                last.then_inc(sk_pe, 1)
                pe.wait_ge(sk_dve, 2 + DS * it + 6)
                for j in range(2):
                    last = nc.tensor.transpose(again[:, j * 128:(j + 1) * 128], laT[:, j, :], ident[:])
                last.then_inc(sk_pe, 1)
            pe.wait_ge(f_lo, 2)
            pe.wait_ge(fo_loaded, 16)

            def expert_up(g, n):
                cols = slice(n * 128, (n + 1) * 128)
                hi, lo = x2T_hi[:, bass.ds(g * FB * S, FB * S)], x2T_lo[:, bass.ds(g * FB * S, FB * S)]
                for i in range(2):
                    fill = 2 * n + i
                    wait(pe, up.drained[fill % 4], up.count(g, fill) - 1)
                    dst = ps[:, up.bank(fill), :]
                    nc.tensor.matmul(dst, w_lo[i][:, cols], hi, start=True, stop=False)
                    nc.tensor.matmul(dst, w_hi[i][:, cols], lo, start=False, stop=False)
                    nc.tensor.matmul(dst, w_hi[i][:, cols], hi, start=False, stop=True).then_inc(up.filled[fill % 4], 1)

            def expert_down(g, e):
                for n in (2 * e, 2 * e + 1):
                    pe.wait_ge(up.drained[(2 * n + 1) % 4], up.count(g, 2 * n + 1))
                wait(pe, down.drained[e % 2], down.count(g, e) - 1)
                for b in range(FB):
                    for n in (2 * e, 2 * e + 1):
                        last = nc.tensor.matmul(ps[:, down.bank(e), b * D:(b + 1) * D], h[n % 4][:, b * S:(b + 1) * S],
                                                wo_sb[:, n, :], start=(n % 2 == 0), stop=(n % 2 == 1))
                last.then_inc(down.filled[e % 2], 1)

            def group(g):
                for e in range(E):
                    expert_up(g, 2 * e)
                    expert_up(g, 2 * e + 1)
                    if e:
                        expert_down(g, e - 1)
                expert_down(g, E - 1)

            groups(pe, group)


def _tables():
    f = np.float32
    tok = np.arange(S, dtype=f)
    inv = f(1.0) / f(6000.0) ** (np.arange(0, ROPE, 2, dtype=f) / f(ROPE))
    ang = np.outer(tok, inv).astype(f)
    cosq = np.concatenate([np.cos(ang)] * 2, axis=1)
    sinq = np.concatenate([-np.sin(ang), np.sin(ang)], axis=1)
    theta = f(10000.0) ** (-np.arange(0, XK, 2, dtype=f) / f(XK))
    xang = (tok[:, None] * theta[None, :]).astype(f)
    xc = np.concatenate([np.cos(xang)] * 2, axis=1)
    xs = np.concatenate([-np.sin(xang), np.sin(xang)], axis=1)
    scale = f(1.0) / np.sqrt(f(XK))
    xcos = np.concatenate([np.tile(xc * scale, (1, XH)), np.tile(xc, (1, XG))], axis=1)
    xsin = np.concatenate([np.tile(xs * scale, (1, XH)), np.tile(xs, (1, XG))], axis=1)
    causal = np.where(np.arange(S)[None, :] > np.arange(S)[:, None], f(CAUSAL), f(0.0))
    eidx = np.tile(np.arange(E, dtype=f) - f(E), (128, 1))
    rows = np.arange(128)
    gsel = rows[:, None] // 32 == np.arange(XG)[None, :]
    return [a.astype(f) for a in (cosq, sinq, xcos, xsin, np.eye(128), causal, gsel, eidx)]


def kernel(**inputs):
    import concourse.bacc as bacc
    from concourse.bass_utils import run_bass_kernel_spmd

    a = {k: np.asarray(v) for k, v in inputs.items()}
    cosq, sinq, xcos, xsin, ident, causal, gsel, eidx = _tables()
    arrays = {
        "x": a["x"], "ctx": a["ctx_1024"],
        "qmask": a["mask_BxS2_bf1"].T, "kpad": a["mask_BxS2_bk0"].T,
        "cosq": cosq, "sinq": sinq, "xcos": xcos, "xsin": xsin, "ident": ident, "causal": causal, "gsel": gsel,
        "wqkv": a["L0_attn_W_qkv"].reshape(QKV, D).T, "wo": a["L0_attn_W_o"].T,
        "xwq": a["L0_xattn_w_q"].reshape(D, XG, GRP, XK).transpose(0, 2, 1, 3).reshape(D, D), "xwkv": np.concatenate([a["L0_xattn_w_k"], a["L0_xattn_w_v"]], axis=1),
        "xwo": a["L0_xattn_w_out"].reshape(XG, GRP, XK, D).transpose(1, 0, 2, 3).reshape(D, D),
        "rw": a["L0_ffn_router_w"].T, "rb": np.broadcast_to(a["L0_ffn_router_b"], (128, E)),
        "temp": np.broadcast_to(a["L0_ffn_temperature"], (128, 1)), "eidx": eidx,
        "fwg": a["L0_ffn_wg"].transpose(1, 0, 2).reshape(D, E * FF),
        "fwp": a["L0_ffn_wp"].transpose(1, 0, 2).reshape(D, E * FF),
        "fwo": a["L0_ffn_wo"].reshape(E * FF, D),
    }
    arrays = {k: np.ascontiguousarray(v) for k, v in arrays.items()}
    nc = bacc.Bacc("TRN2", target_bir_lowering=False, num_devices=1)
    args = [nc.dram_tensor(f"in_{k}", v.shape, mybir.dt.from_np(v.dtype), kind="ExternalInput").ap() for k, v in arrays.items()]
    args.append(nc.dram_tensor("out_y", (B, S, D), F32, kind="ExternalOutput").ap())
    decoder_layer(nc, *args)
    r = run_bass_kernel_spmd(nc, [{f"in_{k}": v for k, v in arrays.items()}], core_ids=[0])
    return r.results[0]["out_y"]
```

```python
from contextlib import ExitStack

import numpy as np
import concourse.bass as bass
from concourse import mybir

F32 = mybir.dt.float32
F32R = mybir.dt.float32r
BF16 = mybir.dt.bfloat16
U8 = mybir.dt.uint8
ALU = mybir.AluOpType
ACT = mybir.ActivationFunctionType
AX_X = mybir.AxisListType.X

B, S, D = 32, 128, 128
H, DK = 16, 64
ROPE = DK // 2
XH, XG, XK = 16, 4, 8
GRP = XH // XG
E, FF = 8, 256
QKV = 3 * H * DK
COLS = 512
CH = H * DK // D
EPS = 1e-5
CAUSAL = -1.0e30
BIG = float(2.0 ** 127)
FB = 4
SINKHORN_ITERS = 3


class Ring:

    def __init__(self, sem, name, banks, fills):
        self.banks = banks
        self.n = len(banks)
        self.per = [len(range(k, fills, self.n)) for k in range(self.n)]
        self.filled = [sem(f"{name}_filled{k}") for k in range(self.n)]
        self.drained = [sem(f"{name}_drained{k}") for k in range(self.n)]

    def bank(self, fill):
        return self.banks[fill % self.n]

    def count(self, b, fill):
        return b * self.per[fill % self.n] + fill // self.n + 1


class SlotRing:

    def __init__(self, sem, order):
        self.order = order
        self.at = {name: i for i, name in enumerate(order)}
        self.filled = [sem(f"bank_filled{k}") for k in range(8)]
        self.drained = [sem(f"bank_drained{k}") for k in range(8)]
        self.first_full = 3

    def bank(self, name):
        return self.at[name] % 8

    def count(self, s, name):
        i = self.at[name]
        if not isinstance(s, int):
            per = len(range(i % 8, len(self.order), 8))
            return s * per + (self.count(self.first_full, name) - per * self.first_full)
        total = 0
        for slot in range(s + 1):
            for j in range(i % 8, len(self.order) if slot < s else i + 1, 8):
                if 0 <= slot - STAGE[self.order[j][0]] < B:
                    total += 1
        return total


STAGE = {"f": 0, "k": 1, "a": 2, "c": 3}


def wait(eng, sem, value):
    if isinstance(value, int) and value <= 0:
        return
    eng.wait_ge(sem, value)


def decoder_layer(nc, x, ctx, qmask, kpad, cosq, sinq, xcos, xsin, ident_d, causal_d, gsel_d, wqkv, wo, xwq, xwkv, xwo,
                  rw, rb, temp, eidx, fwg, fwp, fwo, out):
    with ExitStack() as whole:
        def sem(name):
            return whole.enter_context(nc.semaphore(name))

        def keep(name, shape, dt=F32):
            return whole.enter_context(nc.sbuf_tensor(name, shape, dt))

        ps = whole.enter_context(nc.psum_tensor("ps", [128, 8, COLS], F32))
        x2_all = keep("x2_all", [128, B, D])
        x2T_hi = keep("x2T_hi", [128, B * S], F32R)
        x2T_lo = keep("x2T_lo", [128, B * S], F32R)
        logits = keep("logits", [128, B, E])
        ident = keep("ident", [128, 128])
        mhalf = keep("mhalf", [128, FB])
        scratch = keep("scratch", [128, 1])
        eps = keep("eps", [128, FB])
        temp_sb = keep("temp_sb", [128, 1])
        eidx_sb = keep("eidx_sb", [128, E])

        attention_phase(nc, sem, ps, x2_all, x2T_hi, x2T_lo, logits, ident, mhalf, eps, scratch, x, ctx, qmask, kpad, cosq, sinq,
                        xcos, xsin, ident_d, causal_d, gsel_d, wqkv, wo, xwq, xwkv, xwo, rw, rb,
                        [(temp_sb[:], temp), (eidx_sb[:], eidx)])
        ffn_phase(nc, sem, ps, x2_all, x2T_hi, x2T_lo, logits, ident, mhalf, eps, scratch, temp_sb, eidx_sb, fwg, fwp, fwo, out)


def attention_phase(nc, sem, ps, x2_all, x2T_hi, x2T_lo, logits, ident, mhalf, eps, scratch, x, ctx, qmask, kpad, cosq, sinq,
                    xcos, xsin, ident_d, causal_d, gsel_d, wqkv, wo, xwq, xwkv, xwo, rw, rb, also_loaded):
    with ExitStack() as phase:
        def sb(name, shape, dt=F32):
            return phase.enter_context(nc.sbuf_tensor(name, shape, dt))

        w_hi = sb("w_hi", [128, QKV], F32R)
        w_lo = sb("w_lo", [128, QKV], F32R)
        wo_sb = sb("wo_sb", [128, CH, D])
        xwq_sb = sb("xwq_sb", [128, XH * XK])
        xwkv_sb = sb("xwkv_sb", [128, 2 * XG * XK])
        xwo_sb = sb("xwo_sb", [128, D])
        rw_sb = sb("rw_sb", [128, E])
        rb_sb = sb("rb_sb", [128, E])
        identb = sb("identb", [128, 128], BF16)
        causal = sb("causal", [128, 4, 128], BF16)
        causal_f = sb("causal_f", [128, 128])
        gsel = sb("gsel", [128, XG])
        cos_sb = sb("cos_sb", [128, ROPE])
        sin_sb = sb("sin_sb", [128, ROPE])
        xcos_sb = sb("xcos_sb", [128, XH + XG, XK])
        xsin_sb = sb("xsin_sb", [128, XH + XG, XK])
        qm_u8 = sb("qm_u8", [128, B], U8)
        kp_u8 = sb("kp_u8", [128, B], U8)
        qm_all = sb("qm_all", [128, B])
        kb_all = sb("kb_all", [128, B])
        xf = [sb(f"xf{p}", [128, D]) for p in range(2)]
        xT_hi = sb("xT_hi", [128, S], F32R)
        xT_lo = sb("xT_lo", [128, S], F32R)
        qk = sb("qk", [128, 2 * H, DK])
        qk_sin = sb("qk_sin", [128, 2 * H, ROPE])
        qk_cos = sb("qk_cos", [128, 2 * H, ROPE])
        qT = [sb(f"qT{p}", [128, CH, S]) for p in range(2)]
        kT = [sb(f"kT{p}", [128, CH, S]) for p in range(2)]
        v = [sb(f"v{p}", [128, H * DK]) for p in range(2)]
        prob = sb("prob", [128, 4, 4, S])
        probT = sb("probT", [128, 4, 4, S])
        negmax = sb("negmax", [128, 4, 4])
        sums = sb("sums", [128, 4, 4])
        recip = sb("recip", [128, 4, 4])
        oT = sb("oT", [128, CH, S])
        xres = [sb(f"xres{p}", [128, D]) for p in range(2)]
        y1 = sb("y1", [128, D])
        st1 = sb("st1", [128, 6])
        mv1 = sb("mv1", [128, 2])
        ve1 = sb("ve1", [128, 1])
        rstd1 = sb("rstd1", [128, 1])
        x1 = sb("x1", [128, D])
        x1c = [sb(f"x1c{p}", [128, D]) for p in range(2)]
        cx = [sb(f"cx{p}", [128, D]) for p in range(2)]
        xcT = sb("xcT", [128, 2, S])
        xt1 = sb("xt1", [128, XH + XG, XK])
        xt2 = sb("xt2", [128, XH + XG, XK])
        xr = sb("xr", [128, XH + XG, XK])
        qm = sb("qm", [128, 1])
        xq_pad = sb("xq_pad", [128, GRP, 128], F32R)
        xk_pad = sb("xk_pad", [128, 128], F32R)
        xqT = sb("xqT", [128, GRP, S], F32R)
        xkT = sb("xkT", [128, XG, S], F32R)
        xv = [sb(f"xv{p}", [128, XG, 32]) for p in range(2)]
        xmax = sb("xmax", [128, GRP, XG])
        xprob = sb("xprob", [128, GRP, XG, S])
        xprobT = sb("xprobT", [128, GRP, XG, S])
        xoT = sb("xoT", [128, GRP, S])
        xrec = sb("xrec", [128, GRP, XG])
        xo = sb("xo", [128, XH * XK])
        xonT = sb("xonT", [128, S])
        y2 = sb("y2", [128, D])
        st2 = sb("st2", [128, 6])
        mv2 = sb("mv2", [128, 2])
        ve2 = sb("ve2", [128, 1])
        rstd2 = sb("rstd2", [128, 1])
        x2 = sb("x2", [128, D])
        x2T = sb("x2T", [128, S])

        xq_parts = xq_pad[:].rearrange("p c (g r) -> p (c g) r", g=XG)[:, :, 0:3 * (XK + 1)].rearrange("p h (a k) -> p h a k", a=3)
        xk_parts = xk_pad[:].rearrange("p (g r) -> p g r", g=XG)[:, :, 0:3 * (XK + 1)].rearrange("p g (a k) -> p g a k", a=3)

        ring = SlotRing(sem, [
            "c.PT0", "f.XT", "c.PT1", "c.PT2", "k.S0", "k.S1", "f.Q0", "a.T",
            "c.PT3", "f.Q1", "k.S2", "k.S3", "a.QKV", "k.PT0", "f.Q2", "c.OT",
            "f.Q3", "f.Q4", "k.PT1", "c.O", "f.Q5", "k.PT2", "a.QT", "a.KT",
            "c.T", "f.T0", "k.PT3", "c.Y", "k.OT0", "a.S0", "f.T1", "a.S1",
            "k.OT1", "f.T2", "f.T3", "a.S2", "a.S3", "c.XT", "k.Y", "c.R"])

        w_loaded = sem("w_loaded")
        ident_loaded = sem("ident_loaded")
        wqkv_loaded = [sem(f"wqkv_loaded{half}") for half in range(2)]
        const_ready = sem("const_ready")
        masks_made = sem("masks_made")
        w_hi_ready = sem("w_hi_ready")
        w_lo_ready = [sem(f"w_lo_ready{half}") for half in range(2)]
        xf_loaded = [sem(f"xf_loaded{p}") for p in range(2)]
        xres_loaded = [sem(f"xres_loaded{p}") for p in range(2)]
        cx_loaded = [sem(f"cx_loaded{p}") for p in range(2)]
        x_hi_ready = sem("x_hi_ready")
        sin_done = sem("sin_done")
        cos_done = sem("cos_done")
        roped = sem("roped")
        maxed = sem("maxed")
        summed = sem("summed")
        normed = sem("normed")
        st1_ready = sem("st1_ready")
        mv1_ready = sem("mv1_ready")
        ve1_ready = sem("ve1_ready")
        rstd1_ready = sem("rstd1_ready")
        x1_ready = sem("x1_ready")
        xt_ready = sem("xt_ready")
        xr_ready = sem("xr_ready")
        xhi_ready = sem("xhi_ready")
        xlo_ready = sem("xlo_ready")
        xmaxed = sem("xmaxed")
        xrec_ready = sem("xrec_ready")
        st2_ready = sem("st2_ready")
        mv2_ready = sem("mv2_ready")
        ve2_ready = sem("ve2_ready")
        rstd2_ready = sem("rstd2_ready")
        x2_ready = sem("x2_ready")
        x2_hi_ready = sem("x2_hi_ready")
        x2_split = sem("x2_split")

        small = [(wo_sb[:], wo.rearrange("(c p) n -> p c n", p=128)), (xwq_sb[:], xwq), (xwkv_sb[:], xwkv),
                 (xwo_sb[:], xwo), (rw_sb[:], rw), (rb_sb[:], rb), (cos_sb[:], cosq), (sin_sb[:], sinq),
                 (xcos_sb[:].rearrange("p h k -> p (h k)"), xcos), (xsin_sb[:].rearrange("p h k -> p (h k)"), xsin),
                 (qm_u8[:], qmask), (kp_u8[:], kpad), (causal_f[:], causal_d), (gsel[:], gsel_d)] + also_loaded
        stage = [qk[:].rearrange("p h k -> p (h k)")[:, 0:QKV // 2], prob[:].rearrange("p a b c -> p (a b c)")[:, 0:QKV // 2]]

        def slots(eng, slot):
            for s in range(4):
                slot(s, s % 2, s, s - 1, s - 2, s - 3)
            with eng.Fori(2, B // 2) as turn:
                for p in range(2):
                    s = 2 * turn + p
                    slot(s, p, s, s - 1, s - 2, s - 3)
            for s in range(B, B + 3):
                slot(s, s % 2, s, s - 1, s - 2, s - 3)

        def loads(b, parity):
            return 8 * b + 16 - 8 * parity

        def on(b):
            return not isinstance(b, int) or 0 <= b < B

        def bank(name, n=COLS):
            return ps[:, ring.bank(name), 0:n]

        def filled(eng, s, name):
            eng.wait_ge(ring.filled[ring.bank(name)], ring.count(s, name))

        def drained(eng, s, name):
            eng.wait_ge(ring.drained[ring.bank(name)], ring.count(s, name))

        block = phase.enter_context(nc.Block())

        @block.sync
        def _(sp):
            for half in range(2):
                sp.dma_start(stage[half], wqkv[:, half * QKV // 2:(half + 1) * QKV // 2]).then_inc(wqkv_loaded[half], 16)
                if half == 0:
                    sp.dma_start(ident[:], ident_d).then_inc(ident_loaded, 16)

            def slot(s, p, f, k, a, c):
                q = 1 - p
                if on(f):
                    wait(sp, x_hi_ready, f - 1)
                    sp.dma_start(xf[p][:], x[bass.ds(f, 1), :, :].rearrange("a s d -> s (a d)")).then_inc(xf_loaded[p], 16)
                if isinstance(s, int) and s == 0:
                    for dst, src in small:
                        sp.dma_start(dst, src).then_inc(w_loaded, 16)
                if on(k):
                    wait(sp, st1_ready, k - 1)
                    sp.dma_start(xres[q][:], x[bass.ds(k, 1), :, :].rearrange("a s d -> s (a d)")).then_inc(xres_loaded[q], 16)
                    wait(sp, xt_ready, k - 1)
                    sp.dma_start(cx[q][:], ctx[bass.ds(k, 1), :, :].rearrange("a s d -> s (a d)")).then_inc(cx_loaded[q], 16)

            slots(sp, slot)

        @block.gpsimd
        def _(pool):
            nc.gpsimd.memset(mhalf[:], -0.5)
            nc.gpsimd.memset(eps[:], EPS)
            nc.gpsimd.memset(xq_pad[:].bitcast(F32), 0.0)
            nc.gpsimd.memset(xk_pad[:].bitcast(F32), 0.0)
            for p in range(2):
                nc.gpsimd.memset(xv[p][:], 0.0).then_inc(const_ready, 1)
            pool.wait_ge(const_ready, 2)
            for p in range(2):
                nc.gpsimd.memset(xv[p][:, :, XK:XK + 1], 1.0).then_inc(const_ready, 1)
            part = slice(QKV // 2, QKV)
            pool.wait_ge(w_hi_ready, 2)
            nc.gpsimd.tensor_tensor(w_lo[:, part], stage[1], w_hi[:, part].bitcast(F32),
                                    ALU.subtract).then_inc(w_lo_ready[1], 1)
            pool.wait_ge(w_loaded, 16 * len(small))

            def norm_fill(b, n):
                pool.wait_ge(summed, 4 * b + n + 1)
                nc.gpsimd.tensor_tensor(prob[:, n], prob[:, n], recip[:, n, :, None].broadcast_to([128, 4, S]),
                                        ALU.mult).then_inc(normed, 1)

            def rope_sin(s, n):
                drained(pool, s, f"f.Q{n}")
                part = qk[:, 8 * n:8 * n + 8, 0:ROPE].rearrange("p h (a i) -> p h a i", a=2)
                sines = qk_sin[:, 8 * n:8 * n + 8, :].rearrange("p h (a i) -> p h a i", a=2)
                for side in range(2):
                    table = sin_sb[:, None, side * ROPE // 2:(side + 1) * ROPE // 2].broadcast_to([128, 8, ROPE // 2])
                    last = nc.gpsimd.tensor_tensor(sines[:, :, side, :], part[:, :, 1 - side, :], table, ALU.mult)
                last.then_inc(sin_done, 1)

            def rope_add(b, n):
                pool.wait_ge(sin_done, 4 * b + n + 1)
                pool.wait_ge(cos_done, 4 * b + n + 1)
                nc.gpsimd.tensor_tensor(qk[:, 8 * n:8 * n + 8, 0:ROPE], qk_cos[:, 8 * n:8 * n + 8, :],
                                        qk_sin[:, 8 * n:8 * n + 8, :], ALU.add).then_inc(roped, 1)

            def cross_add(b):
                pool.wait_ge(xt_ready, b + 1)
                nc.gpsimd.tensor_tensor(xr[:], xt1[:], xt2[:], ALU.add).then_inc(xr_ready, 1)

            def rstd(b, mv, ve, out_, mv_ready, ve_ready, done):
                pool.wait_ge(mv_ready, b + 1)
                nc.gpsimd.tensor_tensor(ve[:], mv[:, 1:2], eps[:, 0:1], ALU.add).then_inc(ve_ready, 1)
                pool.wait_ge(ve_ready, b + 1)
                nc.gpsimd.tensor_tensor(out_[:], ve[:], mhalf[:, 0:1], ALU.pow).then_inc(done, 1)

            def slot(s, p, f, k, a, c):
                if on(a):
                    rstd(a, mv1, ve1, rstd1, mv1_ready, ve1_ready, rstd1_ready)
                if on(f):
                    rope_sin(s, 0)
                if on(k):
                    norm_fill(k, 0)
                if on(f):
                    rope_add(f, 0)
                    rope_sin(s, 1)
                if on(k):
                    norm_fill(k, 1)
                if on(a):
                    cross_add(a)
                if on(k):
                    norm_fill(k, 2)
                    norm_fill(k, 3)
                if on(f):
                    rope_sin(s, 2)
                    rope_add(f, 1)
                    rope_sin(s, 3)
                    rope_add(f, 2)
                if on(c):
                    rstd(c, mv2, ve2, rstd2, mv2_ready, ve2_ready, rstd2_ready)
                if on(f):
                    rope_add(f, 3)

            slots(pool, slot)

        @block.scalar
        def _(act):
            def copy(s, name, dst, scale=1.0, n=COLS):
                filled(act, s, name)
                nc.scalar.activation(dst, bank(name, n), ACT.Copy, scale=scale).then_inc(ring.drained[ring.bank(name)], 1)

            for half in range(2):
                act.wait_ge(wqkv_loaded[half], 16)
                nc.scalar.activation(w_hi[:, half * QKV // 2:(half + 1) * QKV // 2], stage[half],
                                     ACT.Copy).then_inc(w_hi_ready, 1)

            def exp_fill(s, b, n):
                name = f"k.S{n}"
                act.wait_ge(maxed, 4 * b + n + 1)
                for j in range(4):
                    last = nc.scalar.activation(prob[:, n, j, :], bank(name)[:, j * S:(j + 1) * S], ACT.Exp,
                                                bias=negmax[:, n, j:j + 1], accum_out=sums[:, n, j:j + 1])
                last.then_inc(ring.drained[ring.bank(name)], 1)

            def xexp_fill(s, b, n):
                name = f"a.S{n}"
                act.wait_ge(xmaxed, 4 * b + n + 1)
                for g in range(XG):
                    last = nc.scalar.activation(xprob[:, n, g, :], bank(name)[:, g * S:(g + 1) * S], ACT.Exp,
                                                bias=xmax[:, n, g:g + 1])
                last.then_inc(ring.drained[ring.bank(name)], 1)

            def q_copy(s, n):
                if isinstance(s, int) and s == 0 and n == 0:
                    act.wait_ge(w_lo_ready[0], 1)
                copy(s, f"f.Q{n}", qk[:, 8 * n:8 * n + 8, :].rearrange("p h k -> p (h k)"), DK ** -0.5 if n < 2 else 1.0)

            def cross_hi(b):
                act.wait_ge(xr_ready, b + 1)
                nc.scalar.activation(xq_parts[:, :, 0:2, 0:XK], xr[:, 0:XH, None, :].broadcast_to([128, XH, 2, XK]),
                                     ACT.Copy, scale=qm[:, 0:1])
                nc.scalar.activation(xk_parts[:, :, 0:3:2, 0:XK], xr[:, XH:XH + XG, None, :].broadcast_to([128, XG, 2, XK]),
                                     ACT.Copy).then_inc(xhi_ready, 1)

            def slot(s, p, f, k, a, c):
                if on(c):
                    copy(s, "c.PT2", xprobT[:, 2].rearrange("p j s -> p (j s)"))
                if on(f):
                    filled(act, s, "f.XT")
                    nc.scalar.activation(xT_hi[:], bank("f.XT", S), ACT.Copy).then_inc(x_hi_ready, 1)
                if on(c):
                    copy(s, "c.PT1", xprobT[:, 1].rearrange("p j s -> p (j s)"))
                if on(f):
                    q_copy(s, 0)
                if on(k):
                    exp_fill(s, k, 0)
                    exp_fill(s, k, 1)
                if on(f):
                    q_copy(s, 1)
                if on(k):
                    exp_fill(s, k, 2)
                    exp_fill(s, k, 3)
                if on(a):
                    cross_hi(a)
                if on(f):
                    q_copy(s, 2)
                    q_copy(s, 3)
                if on(k):
                    copy(s, "k.PT1", probT[:, 1].rearrange("p j s -> p (j s)"))
                if on(f):
                    copy(s, "f.Q5", v[p][:, COLS:2 * COLS])
                if on(c):
                    copy(s, "c.T", xonT[:], n=S)
                if on(k):
                    copy(s, "k.PT2", probT[:, 2].rearrange("p j s -> p (j s)"))
                if on(a):
                    copy(s, "a.QT", xqT[:].rearrange("p c s -> p (c s)"))
                if on(k):
                    copy(s, "k.PT3", probT[:, 3].rearrange("p j s -> p (j s)"))
                if on(f):
                    copy(s, "f.T0", qT[p][:, 0:4, :].rearrange("p c s -> p (c s)"))
                if on(k):
                    copy(s, "k.OT0", oT[:, 0:4, :].rearrange("p c s -> p (c s)"))
                if on(a):
                    xexp_fill(s, a, 0)
                if on(k):
                    copy(s, "k.OT1", oT[:, 4:8, :].rearrange("p c s -> p (c s)"))
                if on(a):
                    xexp_fill(s, a, 1)
                if on(f):
                    copy(s, "f.T3", kT[p][:, 4:8, :].rearrange("p c s -> p (c s)"))
                if on(a):
                    xexp_fill(s, a, 2)
                    xexp_fill(s, a, 3)

            slots(act, slot)

        @block.vector
        def _(dve):
            def copy(s, name, dst, n=COLS):
                filled(dve, s, name)
                nc.vector.tensor_copy(dst, bank(name, n)).then_inc(ring.drained[ring.bank(name)], 1)

            part = slice(0, QKV // 2)
            dve.wait_ge(w_hi_ready, 1)
            nc.vector.tensor_tensor(w_lo[:, part], stage[0], w_hi[:, part].bitcast(F32),
                                    ALU.subtract).then_inc(w_lo_ready[0], 1)

            def make_constants():
                dve.wait_ge(w_loaded, 16 * len(small))
                nc.vector.tensor_copy(qm_all[:], qm_u8[:])
                nc.vector.tensor_copy(identb[:], ident[:])
                nc.vector.tensor_copy(causal[:], causal_f[:, None, :].broadcast_to([128, 4, 128]))
                nc.vector.tensor_scalar(kb_all[:], kp_u8[:], -1.0, BIG, ALU.add, ALU.mult).then_inc(masks_made, 1)
                dve.wait_ge(masks_made, 1)
                dve.wait_ge(const_ready, 4)

            def scores_max(s, name, dst, done):
                filled(dve, s, name)
                nc.vector.tensor_reduce(dst, bank(name).rearrange("p (j s) -> p j s", j=4), AX_X, ALU.max,
                                        negate=True).then_inc(done, 1)

            def recip_fill(s, n):
                drained(dve, s, f"k.S{n}")
                nc.vector.reciprocal(recip[:, n, :], sums[:, n, :]).then_inc(summed, 1)

            def rope_cos(s, n):
                drained(dve, s, f"f.Q{n}")
                nc.vector.tensor_tensor(qk_cos[:, 8 * n:8 * n + 8, :], qk[:, 8 * n:8 * n + 8, 0:ROPE],
                                        cos_sb[:, None, :].broadcast_to([128, 8, ROPE]), ALU.mult).then_inc(cos_done, 1)

            def residual(s, name, y, old, st, done):
                filled(dve, s, name)
                nc.vector.tensor_tensor(y[:], bank(name, D), old[:], ALU.add).then_inc(ring.drained[ring.bank(name)], 1)
                drained(dve, s, name)
                nc.vector.bn_stats(st[:], y[:]).then_inc(done, 1)

            def moments(b, st, mv, st_ready, done):
                dve.wait_ge(st_ready, b + 1)
                nc.vector.memset(scratch[:], 0.0)
                nc.vector.bn_aggr(mv[:], st[:]).then_inc(done, 1)

            def normalise(b, y, mv, rs, dst, kept, rs_ready, done):
                dve.wait_ge(rs_ready, b + 1)
                for d in (dst, kept):
                    last = nc.vector.tensor_scalar(d, y[:], mv[:, 0:1], rs[:, 0:1], ALU.subtract, ALU.mult)
                last.then_inc(done, 1)

            def x_lo(s, b):
                dve.wait_ge(x_hi_ready, b + 1)
                nc.vector.tensor_tensor(xT_lo[:], bank("f.XT", S), xT_hi[:].bitcast(F32),
                                        ALU.subtract).then_inc(ring.drained[ring.bank("f.XT")], 1)

            def cross_k(s):
                filled(dve, s, "a.KT")
                nc.vector.tensor_tensor(xkT[:], bank("a.KT", S)[:, None, :].broadcast_to([128, XG, S]),
                                        gsel[:, :, None].broadcast_to([128, XG, S]), ALU.mult)\
                    .then_inc(ring.drained[ring.bank("a.KT")], 1)

            def divide(s, b):
                filled(dve, s, "c.O")
                o = bank("c.O").rearrange("p (c g r) -> p c g r", c=GRP, g=XG)
                nc.vector.reciprocal(xrec[:], o[:, :, :, XK]).then_inc(xrec_ready, 1)
                dve.wait_ge(xrec_ready, b + 1)
                nc.vector.tensor_tensor(xo[:].rearrange("p (c g k) -> p c g k", g=XG, c=GRP), o[:, :, :, 0:XK],
                                        xrec[:, :, :, None].broadcast_to([128, GRP, XG, XK]), ALU.mult)\
                    .then_inc(ring.drained[ring.bank("c.O")], 1)

            def split_x2(s, b):
                drained(dve, s, "c.XT")
                hi = x2T_hi[:, bass.ds(b * S, S)]
                nc.vector.tensor_copy(hi, x2T[:]).then_inc(x2_hi_ready, 1)
                dve.wait_ge(x2_hi_ready, b + 1)
                nc.vector.tensor_tensor(x2T_lo[:, bass.ds(b * S, S)], x2T[:], hi.bitcast(F32), ALU.subtract).then_inc(x2_split, 1)

            def add_bias(s, b):
                filled(dve, s, "c.R")
                nc.vector.tensor_tensor(logits[:, bass.ds(b, 1), :].rearrange("p a e -> p (a e)"),
                                        bank("c.R", E), rb_sb[:], ALU.add).then_inc(ring.drained[ring.bank("c.R")], 1)

            def cross_rope(s, b, p):
                filled(dve, s, "a.QKV")
                flat = bank("a.QKV", (XH + XG) * XK)
                src = flat.rearrange("p (h a i) -> p h a i", a=2, i=XK // 2)
                nc.vector.tensor_copy(qm[:], qm_all[:, bass.ds(b, 1)])
                nc.vector.tensor_tensor(xt1[:].rearrange("p h k -> p (h k)"), flat, xcos_sb[:].rearrange("p h k -> p (h k)"),
                                        ALU.mult)
                t2 = xt2[:].rearrange("p h (a i) -> p h a i", a=2)
                sn = xsin_sb[:].rearrange("p h (a i) -> p h a i", a=2)
                for side in range(2):
                    last = nc.vector.tensor_tensor(t2[:, :, side, :], src[:, :, 1 - side, :], sn[:, :, side, :], ALU.mult)
                last.then_inc(xt_ready, 1)
                nc.vector.tensor_copy(xv[p][:, :, 0:XK], bank("a.QKV")[:, 160:192].rearrange("p (g k) -> p g k", g=XG))\
                    .then_inc(ring.drained[ring.bank("a.QKV")], 1)

            def cross_lo(b):
                dve.wait_ge(xhi_ready, b + 1)
                nc.vector.scalar_tensor_tensor(xq_parts[:, :, 2, 0:XK], xr[:, 0:XH], qm[:, 0:1],
                                               xq_parts[:, :, 0, 0:XK].bitcast(F32), ALU.mult, ALU.subtract)
                nc.vector.tensor_tensor(xk_parts[:, :, 1, 0:XK], xr[:, XH:XH + XG], xk_parts[:, :, 0, 0:XK].bitcast(F32),
                                        ALU.subtract)
                nc.vector.tensor_copy(xk_parts[:, :, 0, XK], kb_all[:, bass.ds(b, 1)].broadcast_to([128, XG]))
                nc.vector.tensor_copy(xq_parts[:, :, 0, XK], qm[:, 0:1].broadcast_to([128, XH])).then_inc(xlo_ready, 1)

            def slot(s, p, f, k, a, c):
                if on(a):
                    dve.wait_ge(xres_loaded[p], loads(a, p))
                    residual(s - 1, "k.Y", y1, xres[p], st1, st1_ready)
                    moments(a, st1, mv1, st1_ready, mv1_ready)
                if on(c):
                    copy(s, "c.PT0", xprobT[:, 0].rearrange("p j s -> p (j s)"))
                if on(f):
                    x_lo(s, f)
                    if isinstance(s, int) and s == 0:
                        make_constants()
                if on(a):
                    normalise(a, y1, mv1, rstd1, x1[:], x1c[p][:], rstd1_ready, x1_ready)
                if on(k):
                    scores_max(s, "k.S0", negmax[:, 0, :], maxed)
                if on(a):
                    copy(s, "a.T", xcT[:].rearrange("p a s -> p (a s)"), n=2 * S)
                if on(k):
                    scores_max(s, "k.S1", negmax[:, 1, :], maxed)
                if on(f):
                    rope_cos(s, 0)
                if on(c):
                    copy(s, "c.PT3", xprobT[:, 3].rearrange("p j s -> p (j s)"))
                if on(k):
                    recip_fill(s, 0)
                    scores_max(s, "k.S2", negmax[:, 2, :], maxed)
                    scores_max(s, "k.S3", negmax[:, 3, :], maxed)
                    recip_fill(s, 1)
                if on(a):
                    cross_rope(s, a, p)
                if on(f):
                    rope_cos(s, 1)
                if on(k):
                    recip_fill(s, 2)
                if on(c):
                    copy(s, "c.OT", xoT[:].rearrange("p c s -> p (c s)"))
                if on(k):
                    copy(s, "k.PT0", probT[:, 0].rearrange("p j s -> p (j s)"))
                    recip_fill(s, 3)
                if on(f):
                    copy(s, "f.Q4", v[p][:, 0:COLS])
                if on(a):
                    cross_lo(a)
                if on(c):
                    divide(s, c)
                if on(a):
                    cross_k(s)
                if on(f):
                    rope_cos(s, 2)
                    rope_cos(s, 3)
                if on(c):
                    residual(s, "c.Y", y2, x1c[1 - p], st2, st2_ready)
                    moments(c, st2, mv2, st2_ready, mv2_ready)
                if on(a):
                    scores_max(s, "a.S0", xmax[:, 0, :], xmaxed)
                    scores_max(s, "a.S1", xmax[:, 1, :], xmaxed)
                if on(f):
                    copy(s, "f.T1", qT[p][:, 4:8, :].rearrange("p c s -> p (c s)"))
                if on(c):
                    normalise(c, y2, mv2, rstd2, x2[:], x2_all[:, bass.ds(c, 1), :].rearrange("p a d -> p (a d)"), rstd2_ready, x2_ready)
                if on(a):
                    scores_max(s, "a.S2", xmax[:, 2, :], xmaxed)
                if on(c):
                    copy(s, "c.XT", x2T[:], n=S)
                if on(a):
                    scores_max(s, "a.S3", xmax[:, 3, :], xmaxed)
                if on(f):
                    copy(s, "f.T2", kT[p][:, 0:4, :].rearrange("p c s -> p (c s)"))
                if on(c):
                    split_x2(s, c)
                    add_bias(s, c)

            slots(dve, slot)

        @block.tensor
        def _(pe):
            def transpose(dst, src):
                return nc.tensor.transpose(dst, src, ident[:])

            pe.wait_ge(ident_loaded, 16)

            def slot(s, p, f, k, a, c):
                q = 1 - p

                def free(name):
                    wait(pe, ring.drained[ring.bank(name)], ring.count(s, name) - 1)
                    return bank(name)

                def done(name, last):
                    last.then_inc(ring.filled[ring.bank(name)], 1)

                def x_transpose():
                    pe.wait_ge(xf_loaded[p], loads(f, p))
                    done("f.XT", transpose(free("f.XT")[:, 0:S], xf[p][:]))

                def qkv(n):
                    if n == 0:
                        drained(pe, s, "f.XT")
                    if isinstance(s, int) and s == 0 and n in (0, 3):
                        pe.wait_ge(w_lo_ready[n // 3], 1)
                    dst = free(f"f.Q{n}")
                    cols = slice(n * COLS, (n + 1) * COLS)
                    nc.tensor.matmul(dst, xT_hi[:], w_lo[:, cols], start=True, stop=False)
                    nc.tensor.matmul(dst, xT_lo[:], w_hi[:, cols], start=False, stop=False)
                    done(f"f.Q{n}", nc.tensor.matmul(dst, xT_hi[:], w_hi[:, cols], start=False, stop=True))

                def qk_transpose(n):
                    pe.wait_ge(roped, 4 * f + n + 1)
                    dst = free(f"f.T{n}")
                    for j in range(4):
                        last = transpose(dst[:, j * S:(j + 1) * S],
                                         qk[:, 8 * n + 2 * j:8 * n + 2 * j + 2, :].rearrange("p h k -> p (h k)"))
                    done(f"f.T{n}", last)

                def scores(u):
                    names = [f"k.S{2 * u + r}" for r in range(2)]
                    if u == 0:
                        for n in range(4):
                            drained(pe, s - 1, f"f.T{n}")
                    dst = [free(name) for name in names]
                    for r in range(2):
                        nc.tensor.matmul(dst[r], identb[:], causal[:].rearrange("p j s -> p (j s)"), start=True, stop=False,
                                         skip_group_check=True)
                    for j in range(4):
                        for r in range(2):
                            rows = slice(64 * r, 64 * r + 64)
                            last = nc.tensor.matmul(dst[r][:, j * S:(j + 1) * S], qT[q][rows, 4 * u + j, :],
                                                    kT[q][rows, 4 * u + j, :], start=False, stop=(j == 3),
                                                    skip_group_check=True)
                            if j == 3:
                                done(names[r], last)

                def prob_transpose(n):
                    pe.wait_ge(normed, 4 * k + n + 1)
                    dst = free(f"k.PT{n}")
                    for j in range(4):
                        last = transpose(dst[:, j * S:(j + 1) * S], prob[:, n, j, :])
                    done(f"k.PT{n}", last)

                def pv(u):
                    for r in range(2):
                        drained(pe, s, f"k.PT{2 * u + r}")
                    dst = free(f"k.OT{u}")
                    for j in range(4):
                        for r in range(2):
                            h = 2 * (4 * u + j) + r
                            last = nc.tensor.matmul(dst[64 * r:64 * r + 64, j * S:(j + 1) * S],
                                                    v[q][:, h * DK:(h + 1) * DK], probT[:, 2 * u + r, j, :],
                                                    start=True, stop=True)
                    done(f"k.OT{u}", last)

                def out_proj():
                    for u in range(2):
                        drained(pe, s, f"k.OT{u}")
                    dst = free("k.Y")
                    for n in range(CH):
                        last = nc.tensor.matmul(dst[:, 0:D], oT[:, n, :], wo_sb[:, n, :], start=(n == 0), stop=(n == CH - 1))
                    done("k.Y", last)

                def xc_transpose():
                    pe.wait_ge(x1_ready, a + 1)
                    pe.wait_ge(cx_loaded[p], loads(a, p))
                    dst = free("a.T")
                    transpose(dst[:, 0:S], x1[:])
                    done("a.T", transpose(dst[:, S:2 * S], cx[p][:]))

                def xqkv():
                    drained(pe, s, "a.T")
                    dst = free("a.QKV")
                    nc.tensor.matmul(dst[:, 0:128], xcT[:, 0, :], xwq_sb[:], start=True, stop=True)
                    done("a.QKV", nc.tensor.matmul(dst[:, 128:192], xcT[:, 1, :], xwkv_sb[:], start=True, stop=True))

                def xqk_transpose():
                    pe.wait_ge(xlo_ready, a + 1)
                    dst = free("a.QT")
                    for j in range(GRP):
                        last = transpose(dst[:, j * S:(j + 1) * S], xq_pad[:, j].bitcast(F32))
                    done("a.QT", last)
                    done("a.KT", transpose(free("a.KT")[:, 0:S], xk_pad[:].bitcast(F32)))

                def xscores(n):
                    if n == 0:
                        drained(pe, s, "a.QT")
                        drained(pe, s, "a.KT")
                    done(f"a.S{n}", nc.tensor.matmul(free(f"a.S{n}"), xqT[:, n, :], xkT[:].rearrange("p g s -> p (g s)"),
                                                     start=True, stop=True))

                def xprob_transpose(n):
                    drained(pe, s - 1, f"a.S{n}")
                    dst = free(f"c.PT{n}")
                    for g in range(XG):
                        last = transpose(dst[:, g * S:(g + 1) * S], xprob[:, n, g, :])
                    done(f"c.PT{n}", last)

                def xpv():
                    for n in range(4):
                        drained(pe, s, f"c.PT{n}")
                    dst = free("c.OT")
                    for g in range(XG):
                        last = nc.tensor.matmul(dst[32 * g:32 * g + 32, :], xv[q][:, g, :], xprobT[:, :, g, :],
                                                start=True, stop=True, skip_group_check=True)
                    done("c.OT", last)

                def xo_back():
                    drained(pe, s, "c.OT")
                    dst = free("c.O")
                    for j in range(GRP):
                        last = transpose(dst[:, j * S:(j + 1) * S], xoT[:, j, :])
                    done("c.O", last)

                def xo_transpose():
                    drained(pe, s, "c.O")
                    done("c.T", transpose(free("c.T")[:, 0:S], xo[:]))

                def xout():
                    drained(pe, s, "c.T")
                    done("c.Y", nc.tensor.matmul(free("c.Y")[:, 0:D], xonT[:], xwo_sb[:], start=True, stop=True))

                def x2_transpose():
                    pe.wait_ge(x2_ready, c + 1)
                    done("c.XT", transpose(free("c.XT")[:, 0:S], x2[:]))

                def router():
                    drained(pe, s, "c.XT")
                    done("c.R", nc.tensor.matmul(free("c.R")[:, 0:E], x2T[:], rw_sb[:], start=True, stop=True))

                if isinstance(s, int) and s == 1:
                    pe.wait_ge(w_loaded, 16 * len(small))
                    pe.wait_ge(masks_made, 1)
                    pe.wait_ge(const_ready, 4)
                if on(c):
                    xprob_transpose(0)
                if on(f):
                    x_transpose()
                if on(c):
                    xprob_transpose(1)
                    xprob_transpose(2)
                if on(k):
                    scores(0)
                if on(f):
                    qkv(0)
                if on(a):
                    xc_transpose()
                if on(c):
                    xprob_transpose(3)
                if on(f):
                    qkv(1)
                if on(k):
                    scores(1)
                if on(a):
                    xqkv()
                if on(k):
                    prob_transpose(0)
                if on(f):
                    qkv(2)
                if on(c):
                    xpv()
                if on(f):
                    qkv(3)
                    qkv(4)
                if on(k):
                    prob_transpose(1)
                if on(c):
                    xo_back()
                if on(f):
                    qkv(5)
                if on(k):
                    prob_transpose(2)
                if on(a):
                    xqk_transpose()
                if on(c):
                    xo_transpose()
                if on(f):
                    qk_transpose(0)
                if on(k):
                    prob_transpose(3)
                if on(c):
                    xout()
                if on(k):
                    pv(0)
                if on(a):
                    xscores(0)
                if on(f):
                    qk_transpose(1)
                if on(a):
                    xscores(1)
                if on(k):
                    pv(1)
                if on(f):
                    qk_transpose(2)
                    qk_transpose(3)
                if on(a):
                    xscores(2)
                    xscores(3)
                if on(c):
                    x2_transpose()
                if on(k):
                    out_proj()
                if on(c):
                    router()

            slots(pe, slot)


def ffn_phase(nc, sem, ps, x2_all, x2T_hi, x2T_lo, logits, ident, mhalf, eps, scratch, temp_sb, eidx_sb, fwg, fwp, fwo, out):
    NF = E * FF // 128
    with ExitStack() as phase:
        def sb(name, shape, dt=F32):
            return phase.enter_context(nc.sbuf_tensor(name, shape, dt))

        stage = [sb(f"fstage{i}", [128, E * FF]) for i in range(2)]
        w_hi = [sb(f"fw_hi{i}", [128, E * FF], F32R) for i in range(2)]
        w_lo = [sb(f"fw_lo{i}", [128, E * FF], F32R) for i in range(2)]
        wo_sb = sb("fwo_sb", [128, NF, D])
        rtemp = sb("rtemp", [128, 2])
        la = sb("la", [128, B, E])
        laT = sb("laT", [128, 2, S])
        dif = sb("dif", [128, B, E])
        ex = sb("ex", [128, B, E])
        exT = sb("exT", [128, 2, S])
        rmax = sb("rmax", [128, B])
        rsum = sb("rsum", [128, B])
        rlog = sb("rlog", [128, B])
        cmax = sb("cmax", [128, 2])
        csum = sb("csum", [128, 2])
        clog = sb("clog", [128, 2])
        gates = sb("gates", [128, B, E])
        cand = sb("cand", [128, B, E])
        one = [sb(f"one{i}", [128, B, E]) for i in range(2)]
        top = [sb(f"top{i}", [128, B]) for i in range(2)]
        low = sb("low", [128, B])
        wts = sb("wts", [128, B, E])
        gs = [sb(f"gs{i}", [128, FB * S]) for i in range(2)]
        h = [sb(f"h{i}", [128, FB * S]) for i in range(4)]
        part = [sb(f"part{i}", [128, FB, D]) for i in range(2)]
        acc = sb("acc", [128, FB, D])
        st3 = sb("st3", [128, FB, 6])
        mv3 = sb("mv3", [128, FB, 2])
        ve3 = sb("ve3", [128, FB])
        rstd3 = sb("rstd3", [128, FB])
        yo = sb("yo", [128, FB, D])

        up = Ring(sem, "up", [0, 1, 2, 3], 2 * NF)
        down = Ring(sem, "down", [4, 5], E)
        f_loaded = sem("f_loaded")
        fo_loaded = sem("fo_loaded")
        f_hi = sem("f_hi")
        f_lo = sem("f_lo")
        sk_dve = sem("sk_dve")
        sk_act = sem("sk_act")
        sk_scaled = sem("sk_scaled")
        sk_pe = sem("sk_pe")
        acc_done = sem("acc_done")
        st3_ready = sem("st3_ready")
        mv3_ready = sem("mv3_ready")
        ve3_ready = sem("ve3_ready")
        rstd3_ready = sem("rstd3_ready")
        yo_ready = sem("yo_ready")
        stored = sem("stored")

        there, again = ps[:, 6, 0:2 * S], ps[:, 7, 0:2 * S]
        flat = lambda t: t[:].rearrange("p b e -> p (b e)")
        over_e = lambda t: t[:, :, None].broadcast_to([128, B, E])

        def groups(eng, group):
            group(0)
            with eng.Fori(1, B // FB) as g:
                group(g)

        def later(g):
            return not isinstance(g, int) or g > 0

        EARLY_PE, EARLY_DVE = 4, 6
        HALVES = [(i, slice(half * E * FF // 2, (half + 1) * E * FF // 2)) for half in range(2) for i in range(2)]

        DS, AS, PS = 6, 4, 2

        block = phase.enter_context(nc.Block())

        @block.sync
        def _(sp):
            sp.dma_start(stage[0][:], fwg).then_inc(f_loaded, 16)
            sp.dma_start(stage[1][:], fwp).then_inc(f_loaded, 16)
            sp.dma_start(wo_sb[:], fwo.rearrange("(n p) d -> p n d", p=128)).then_inc(fo_loaded, 16)

            def group(g):
                sp.wait_ge(yo_ready, FB * (g + 1))
                sp.dma_start(out[bass.ds(g * FB, FB), :, :].rearrange("a s d -> s a d"), yo[:]).then_inc(stored, 16)

            groups(sp, group)
            sp.wait_ge(stored, 16 * (B // FB))

        @block.gpsimd
        def _(pool):
            for n, (i, cols) in enumerate(HALVES):
                pool.wait_ge(f_hi, n + 1)
                nc.gpsimd.tensor_tensor(w_lo[i][:, cols], stage[i][:, cols], w_hi[i][:, cols].bitcast(F32),
                                        ALU.subtract).then_inc(f_lo, 1)

            def accumulate(g, e):
                pool.wait_ge(down.drained[e % 2], down.count(g, e))
                pool.wait_ge(acc_done, (E + 1) * g + e + 1)
                nc.gpsimd.tensor_tensor(acc[:], acc[:], part[e % 2][:], ALU.add).then_inc(acc_done, 1)

            def finish(g):
                accumulate(g, E - 1)
                pool.wait_ge(mv3_ready, FB * (g + 1))
                nc.gpsimd.tensor_tensor(ve3[:], mv3[:, :, 1], eps[:], ALU.add).then_inc(ve3_ready, 1)
                pool.wait_ge(ve3_ready, g + 1)
                nc.gpsimd.tensor_tensor(rstd3[:], ve3[:], mhalf[:], ALU.pow).then_inc(rstd3_ready, 1)

            def group(g):
                if later(g):
                    finish(g - 1)
                wait(pool, yo_ready, FB * g)
                own = x2_all[:, bass.ds(g * FB, FB), :]
                nc.gpsimd.tensor_tensor(acc[:], own, own, ALU.add).then_inc(acc_done, 1)
                for e in range(E - 1):
                    accumulate(g, e)

            groups(pool, group)
            finish(B // FB - 1)

        @block.scalar
        def _(act):
            def split(n):
                i, cols = HALVES[n]
                act.wait_ge(f_loaded, 32)
                nc.scalar.activation(w_hi[i][:, cols], stage[i][:, cols], ACT.Copy).then_inc(f_hi, 1)

            def relu(g, n):
                act.wait_ge(up.filled[(2 * n) % 4], up.count(g, 2 * n))
                wait(act, up.drained[(2 * n + 1) % 4], up.count(g, 2 * n + 1) - 1)
                nc.scalar.activation(gs[n % 2][:], ps[:, up.bank(2 * n), :], ACT.Relu).then_inc(up.drained[(2 * n) % 4], 1)

            for it in range(SINKHORN_ITERS):
                act.wait_ge(sk_dve, 2 + DS * it + 2)
                nc.scalar.activation(flat(ex), flat(dif), ACT.Exp).then_inc(sk_act, 1)
                act.wait_ge(sk_dve, 2 + DS * it + 3)
                nc.scalar.activation(rlog[:], rsum[:], ACT.Ln).then_inc(sk_act, 1)
                if it == SINKHORN_ITERS - 1:
                    relu(0, 0)
                    relu(0, 1)
                act.wait_ge(sk_dve, 2 + DS * it + 5)
                for j in range(2):
                    last = nc.scalar.activation(exT[:, j, :], there[:, j * S:(j + 1) * S], ACT.Exp, bias=cmax[:, j:j + 1],
                                                accum_out=csum[:, j:j + 1])
                last.then_inc(sk_act, 1)
                act.wait_ge(sk_act, AS * it + 3)
                nc.scalar.activation(clog[:], csum[:], ACT.Ln).then_inc(sk_act, 1)
                if it < 2:
                    split(2 * it)
                    split(2 * it + 1)
                if it == SINKHORN_ITERS - 1:
                    relu(0, 2)
                    relu(0, 3)
            act.wait_ge(sk_pe, PS * SINKHORN_ITERS)
            nc.scalar.activation(flat(ex), again, ACT.Exp).then_inc(sk_act, 1)

            def group(g):
                for n in range(0 if later(g) else EARLY_PE, NF):
                    relu(g, n)

            groups(act, group)

        @block.vector
        def _(dve):
            steps = [0]

            def link(ins):
                steps[0] += 1
                ins.then_inc(sk_dve, 1)
                dve.wait_ge(sk_dve, steps[0])

            first, others = slice(0, FB), slice(FB, B)

            def spread(t, r):
                return t[:, r, None].broadcast_to([128, r.stop - r.start, E])

            def gates_of(r):
                link(nc.vector.tensor_reduce(rsum[:, r], ex[:, r], AX_X, ALU.add))
                link(nc.vector.tensor_scalar(rlog[:, r], rsum[:, r], 1e-8, None, ALU.add))
                link(nc.vector.reciprocal(rmax[:, r], rlog[:, r]))
                link(nc.vector.tensor_tensor(gates[:, r], ex[:, r], spread(rmax, r), ALU.mult))

            def top_expert(r, i):
                src = gates if i == 0 else dif
                idx = eidx_sb[:, None, :].broadcast_to([128, r.stop - r.start, E])
                link(nc.vector.tensor_reduce(top[i][:, r], src[:, r], AX_X, ALU.max))
                link(nc.vector.tensor_tensor(cand[:, r], src[:, r], spread(top[i], r), ALU.is_equal))
                link(nc.vector.tensor_tensor(cand[:, r], cand[:, r], idx, ALU.mult))
                link(nc.vector.tensor_reduce(low[:, r], cand[:, r], AX_X, ALU.min))
                link(nc.vector.tensor_tensor(one[i][:, r], cand[:, r], spread(low, r), ALU.is_equal))
                if i == 0:
                    link(nc.vector.scalar_tensor_tensor(dif[:, r], one[0][:, r], -4.0, gates[:, r], ALU.mult, ALU.add))

            def weights_of(r):
                link(nc.vector.scalar_tensor_tensor(rsum[:, r], top[0][:, r], 1e-8, top[1][:, r], ALU.add, ALU.add))
                link(nc.vector.reciprocal(rlog[:, r], rsum[:, r]))
                link(nc.vector.tensor_tensor(cand[:, r], one[0][:, r], one[1][:, r], ALU.add))
                link(nc.vector.tensor_tensor(one[0][:, r], cand[:, r], gates[:, r], ALU.mult))
                link(nc.vector.tensor_tensor(wts[:, r], one[0][:, r], spread(rlog, r), ALU.mult))

            def hidden(g, n):
                dve.wait_ge(up.filled[(2 * n + 1) % 4], up.count(g, 2 * n + 1))
                dve.wait_ge(up.drained[(2 * n) % 4], up.count(g, 2 * n))
                if n % 2 == 0:
                    wait(dve, down.filled[(n // 2) % 2], down.count(g, n // 2) - 1)
                nc.vector.tensor_tensor(h[n % 4][:], ps[:, up.bank(2 * n + 1), :], gs[n % 2][:], ALU.mult)\
                    .then_inc(up.drained[(2 * n + 1) % 4], 1)

            link(nc.vector.tensor_scalar(rtemp[:, 0:1], temp_sb[:], 0.1, None, ALU.max))
            link(nc.vector.reciprocal(rtemp[:, 1:2], rtemp[:, 0:1]))
            sc_step = nc.vector.tensor_scalar(flat(la), flat(logits), rtemp[:, 1:2], None, ALU.mult)
            for it in range(SINKHORN_ITERS):
                if it == 0:
                    sc_step.then_inc(sk_scaled, 1)
                    dve.wait_ge(sk_scaled, 1)
                    src = la[:]
                else:
                    dve.wait_ge(sk_pe, PS * it)
                    src = again.rearrange("p (b e) -> p b e", b=B)
                link(nc.vector.tensor_reduce(rmax[:], src, AX_X, ALU.max))
                link(nc.vector.tensor_tensor(dif[:], src, over_e(rmax), ALU.subtract))
                dve.wait_ge(sk_act, AS * it + 1)
                link(nc.vector.tensor_reduce(rsum[:], ex[:], AX_X, ALU.add))
                dve.wait_ge(sk_act, AS * it + 2)
                link(nc.vector.tensor_tensor(la[:], dif[:], over_e(rlog), ALU.subtract))
                dve.wait_ge(sk_pe, PS * it + 1)
                link(nc.vector.tensor_reduce(cmax[:], there.rearrange("p (j s) -> p j s", j=2), AX_X, ALU.max, negate=True))
                if it == SINKHORN_ITERS - 1:
                    hidden(0, 0)
                    hidden(0, 1)
                dve.wait_ge(sk_act, AS * it + 4)
                for j in range(2):
                    last = nc.vector.tensor_scalar(laT[:, j, :], there[:, j * S:(j + 1) * S], cmax[:, j:j + 1],
                                                   clog[:, j:j + 1], ALU.add, ALU.subtract)
                link(last)
            hidden(0, 2)
            hidden(0, 3)
            dve.wait_ge(sk_act, AS * SINKHORN_ITERS + 1)
            gates_of(first)
            top_expert(first, 0)
            hidden(0, 4)
            hidden(0, 5)
            top_expert(first, 1)
            weights_of(first)

            def combine(g, e):
                dve.wait_ge(down.filled[e % 2], down.count(g, e))
                wait(dve, acc_done, (E + 1) * g + (e if e >= 2 else e - 1))
                nc.vector.tensor_tensor(part[e % 2][:], ps[:, down.bank(e), :].rearrange("p (b d) -> p b d", b=FB),
                                        wts[:, bass.ds(g * FB, FB), e:e + 1].broadcast_to([128, FB, D]), ALU.mult)\
                    .then_inc(down.drained[e % 2], 1)

            def moments(g):
                dve.wait_ge(acc_done, (E + 1) * (g + 1))
                for b in range(FB):
                    nc.vector.bn_stats(st3[:, b, :], acc[:, b, :]).then_inc(st3_ready, 1)
                dve.wait_ge(st3_ready, FB * (g + 1))
                nc.vector.memset(scratch[:], 0.0)
                for b in range(FB):
                    nc.vector.bn_aggr(mv3[:, b, :], st3[:, b, :]).then_inc(mv3_ready, 1)

            def normalise(g):
                dve.wait_ge(rstd3_ready, g + 1)
                wait(dve, stored, 16 * g)
                for b in range(FB):
                    nc.vector.tensor_scalar(yo[:, b, :], acc[:, b, :], mv3[:, b, 0:1], rstd3[:, b:b + 1],
                                            ALU.subtract, ALU.mult).then_inc(yo_ready, 1)

            def group(g):
                for e in range(E):
                    for n in (2 * e, 2 * e + 1):
                        if later(g) or n >= EARLY_DVE:
                            hidden(g, n)
                    if e:
                        combine(g, e - 1)
                    if not later(g):
                        if e == 3:
                            gates_of(others)
                        if e == 4:
                            top_expert(others, 0)
                        if e == 5:
                            top_expert(others, 1)
                        if e == 6:
                            weights_of(others)
                    if later(g):
                        if e == 0:
                            combine(g - 1, E - 1)
                        if e == 1:
                            moments(g - 1)
                        if e == 2:
                            normalise(g - 1)

            groups(dve, group)
            combine(B // FB - 1, E - 1)
            moments(B // FB - 1)
            normalise(B // FB - 1)

        @block.tensor
        def _(pe):
            def expert_up(g, n):
                if not later(g) and n in (0, NF // 2):
                    pe.wait_ge(f_lo, 2 if n == 0 else 4)
                cols = slice(n * 128, (n + 1) * 128)
                hi, lo = x2T_hi[:, bass.ds(g * FB * S, FB * S)], x2T_lo[:, bass.ds(g * FB * S, FB * S)]
                for i in range(2):
                    fill = 2 * n + i
                    wait(pe, up.drained[fill % 4], up.count(g, fill) - 1)
                    dst = ps[:, up.bank(fill), :]
                    nc.tensor.matmul(dst, w_lo[i][:, cols], hi, start=True, stop=False)
                    nc.tensor.matmul(dst, w_hi[i][:, cols], lo, start=False, stop=False)
                    nc.tensor.matmul(dst, w_hi[i][:, cols], hi, start=False, stop=True).then_inc(up.filled[fill % 4], 1)

            def expert_down(g, e):
                for n in (2 * e, 2 * e + 1):
                    pe.wait_ge(up.drained[(2 * n + 1) % 4], up.count(g, 2 * n + 1))
                wait(pe, down.drained[e % 2], down.count(g, e) - 1)
                for b in range(FB):
                    for n in (2 * e, 2 * e + 1):
                        last = nc.tensor.matmul(ps[:, down.bank(e), b * D:(b + 1) * D], h[n % 4][:, b * S:(b + 1) * S],
                                                wo_sb[:, n, :], start=(n % 2 == 0), stop=(n % 2 == 1))
                last.then_inc(down.filled[e % 2], 1)

            for it in range(SINKHORN_ITERS):
                pe.wait_ge(sk_dve, 2 + DS * it + 4)
                for j in range(2):
                    last = nc.tensor.transpose(there[:, j * S:(j + 1) * S], flat(la)[:, j * 128:(j + 1) * 128], ident[:])
                last.then_inc(sk_pe, 1)
                if it == SINKHORN_ITERS - 1:
                    expert_up(0, 2)
                    expert_up(0, 3)
                pe.wait_ge(sk_dve, 2 + DS * it + 6)
                for j in range(2):
                    last = nc.tensor.transpose(again[:, j * 128:(j + 1) * 128], laT[:, j, :], ident[:])
                last.then_inc(sk_pe, 1)
                if it == SINKHORN_ITERS - 2:
                    expert_up(0, 0)
                    expert_up(0, 1)
            pe.wait_ge(fo_loaded, 16)

            def group(g):
                for e in range(E):
                    for n in (2 * e, 2 * e + 1):
                        if later(g) or n >= EARLY_PE:
                            expert_up(g, n)
                    if e:
                        expert_down(g, e - 1)
                    elif later(g):
                        expert_down(g - 1, E - 1)

            groups(pe, group)
            expert_down(B // FB - 1, E - 1)


def _tables():
    f = np.float32
    tok = np.arange(S, dtype=f)
    inv = f(1.0) / f(6000.0) ** (np.arange(0, ROPE, 2, dtype=f) / f(ROPE))
    ang = np.outer(tok, inv).astype(f)
    cosq = np.concatenate([np.cos(ang)] * 2, axis=1)
    sinq = np.concatenate([-np.sin(ang), np.sin(ang)], axis=1)
    theta = f(10000.0) ** (-np.arange(0, XK, 2, dtype=f) / f(XK))
    xang = (tok[:, None] * theta[None, :]).astype(f)
    xc = np.concatenate([np.cos(xang)] * 2, axis=1)
    xs = np.concatenate([-np.sin(xang), np.sin(xang)], axis=1)
    scale = f(1.0) / np.sqrt(f(XK))
    xcos = np.concatenate([np.tile(xc * scale, (1, XH)), np.tile(xc, (1, XG))], axis=1)
    xsin = np.concatenate([np.tile(xs * scale, (1, XH)), np.tile(xs, (1, XG))], axis=1)
    causal = np.where(np.arange(S)[None, :] > np.arange(S)[:, None], f(CAUSAL), f(0.0))
    eidx = np.tile(np.arange(E, dtype=f) - f(E), (128, 1))
    rows = np.arange(128)
    gsel = rows[:, None] // 32 == np.arange(XG)[None, :]
    return [a.astype(f) for a in (cosq, sinq, xcos, xsin, np.eye(128), causal, gsel, eidx)]


def kernel(**inputs):
    import concourse.bacc as bacc
    from concourse.bass_utils import run_bass_kernel_spmd

    a = {k: np.asarray(v) for k, v in inputs.items()}
    cosq, sinq, xcos, xsin, ident, causal, gsel, eidx = _tables()
    arrays = {
        "x": a["x"], "ctx": a["ctx_1024"],
        "qmask": a["mask_BxS2_bf1"].T, "kpad": a["mask_BxS2_bk0"].T,
        "cosq": cosq, "sinq": sinq, "xcos": xcos, "xsin": xsin, "ident": ident, "causal": causal, "gsel": gsel,
        "wqkv": a["L0_attn_W_qkv"].reshape(QKV, D).T, "wo": a["L0_attn_W_o"].T,
        "xwq": a["L0_xattn_w_q"].reshape(D, XG, GRP, XK).transpose(0, 2, 1, 3).reshape(D, D), "xwkv": np.concatenate([a["L0_xattn_w_k"], a["L0_xattn_w_v"]], axis=1),
        "xwo": a["L0_xattn_w_out"].reshape(XG, GRP, XK, D).transpose(1, 0, 2, 3).reshape(D, D),
        "rw": a["L0_ffn_router_w"].T, "rb": np.broadcast_to(a["L0_ffn_router_b"], (128, E)),
        "temp": np.broadcast_to(a["L0_ffn_temperature"], (128, 1)), "eidx": eidx,
        "fwg": a["L0_ffn_wg"].transpose(1, 0, 2).reshape(D, E * FF),
        "fwp": a["L0_ffn_wp"].transpose(1, 0, 2).reshape(D, E * FF),
        "fwo": a["L0_ffn_wo"].reshape(E * FF, D),
    }
    arrays = {k: np.ascontiguousarray(v) for k, v in arrays.items()}
    nc = bacc.Bacc("TRN2", target_bir_lowering=False, num_devices=1)
    args = [nc.dram_tensor(f"in_{k}", v.shape, mybir.dt.from_np(v.dtype), kind="ExternalInput").ap() for k, v in arrays.items()]
    args.append(nc.dram_tensor("out_y", (B, S, D), F32, kind="ExternalOutput").ap())
    decoder_layer(nc, *args)
    r = run_bass_kernel_spmd(nc, [{f"in_{k}": v for k, v in arrays.items()}], core_ids=[0])
    return r.results[0]["out_y"]
```
